# Optimizing a Trainium2 kernel written in Bass

```python
import numpy as np
import jax
import jax.numpy as jnp

def _softmax(x, axis=-1):
    return jax.nn.softmax(x, axis=axis)

def _gelu(x):
    return jax.nn.gelu(x, approximate=True)

def _silu(x):
    return jax.nn.silu(x)

def _sigmoid(x):
    return jax.nn.sigmoid(x)

def _layernorm(x, axis=-1, eps=1e-05):
    m = jnp.mean(x, axis=axis, keepdims=True)
    v = jnp.var(x, axis=axis, keepdims=True)
    return (x - m) / jnp.sqrt(v + eps)

def _scatter_add(tgt, idx, src, axis=0):
    return tgt.at[idx].add(src)

def _segment_sum(src, seg, n):
    return jax.ops.segment_sum(src, seg, n)
kernel_name = 'mk_gnn_preln_d1_gnn_r32_d9c630'

def setup_inputs(seed: int=0):
    np.random.seed(seed)
    _w = jnp.asarray

    def _rec_inputs():
        import jax
        import jax.numpy as jnp
        _gk = jax.random.key(seed)
        x = -0.0003542 + 1 * jax.random.normal(jax.random.fold_in(_gk, 1), (500, 256), jnp.float32)
        _s = jax.random.randint(jax.random.fold_in(_gk, 2), (8000,), 0, 500, jnp.int32)
        _d = jax.random.randint(jax.random.fold_in(_gk, 3), (8000,), 0, 500, jnp.int32)
        _loop = jnp.arange(500, dtype=jnp.int32)
        src = jnp.concatenate([_s, _d, _loop])
        dst = jnp.concatenate([_d, _s, _loop])
        _o = jnp.argsort(dst, stable=True)
        src = src[_o]
        dst = dst[_o]
        edge_attr_128 = 4.82035e-05 + 0.999966 * jax.random.normal(jax.random.fold_in(_gk, 11), (16500, 128), jnp.float32)
        edge_weight = jax.random.uniform(jax.random.fold_in(_gk, 13), (16500,), jnp.float32, 0.0, 0.999951)
        return (x, src, dst, edge_attr_128, edge_weight)
    x, src, dst, edge_attr_128, edge_weight = _rec_inputs()

    def _L0_gnn_setup():
        import jax, jax.numpy as jnp
        import numpy as np
        BN_EPS = 1e-05

        def _bn(x, gamma, beta, mean, var):
            return (x - mean) / jnp.sqrt(var + BN_EPS) * gamma + beta
        key = jax.random.key(seed)
        ks = jax.random.split(key, 24)
        N, E = (500, 2000)
        D_IN, H, D_OUT, D_E, KH = (256, 64, 256, 128, 32)
        s = 0.05
        inp = {}
        inp['x'] = jax.random.normal(ks[0], (N, D_IN), jnp.float32)
        inp['edge_input'] = jax.random.normal(ks[1], (E, D_E), jnp.float32)
        inp['edge_list'] = jax.random.randint(ks[2], (E, 2), 0, N, jnp.int32)
        inp['edge_weight'] = jax.random.uniform(ks[3], (E,), jnp.float32)
        inp['w1'] = jax.random.normal(ks[4], (D_IN, H), jnp.float32) * s
        inp['b1'] = jax.random.normal(ks[5], (H,), jnp.float32) * s
        inp['kw1'] = jax.random.normal(ks[6], (D_E, KH), jnp.float32) * s
        inp['kb1'] = jax.random.normal(ks[7], (KH,), jnp.float32) * s
        inp['kw2'] = jax.random.normal(ks[8], (KH, (H + 1) * H), jnp.float32) * s
        inp['kb2'] = jax.random.normal(ks[9], ((H + 1) * H,), jnp.float32) * s
        inp['w2'] = jax.random.normal(ks[10], (H, D_OUT), jnp.float32) * s
        inp['b2'] = jax.random.normal(ks[11], (D_OUT,), jnp.float32) * s

        def bn_params(k, d):
            k1, k2, k3, k4 = jax.random.split(k, 4)
            g = 1.0 + jax.random.normal(k1, (d,), jnp.float32) * s
            b = jax.random.normal(k2, (d,), jnp.float32) * s
            m = jax.random.normal(k3, (d,), jnp.float32) * s
            v = 0.5 + jax.random.uniform(k4, (d,), jnp.float32)
            return (g, b, m, v)
        inp['g_in'], inp['be_in'], inp['m_in'], inp['v_in'] = bn_params(ks[12], D_IN)
        inp['g_msg'], inp['be_msg'], inp['m_msg'], inp['v_msg'] = bn_params(ks[13], H)
        inp['g_upd'], inp['be_upd'], inp['m_upd'], inp['v_upd'] = bn_params(ks[14], H)
        inp['g_out'], inp['be_out'], inp['m_out'], inp['v_out'] = bn_params(ks[15], D_OUT)
        return inp
    _L0_gnn_all = _L0_gnn_setup()
    _L0_gnn_in = {k: v for k, v in _L0_gnn_all.items() if k in ('w1', 'b1', 'kw1', 'kb1', 'kw2', 'kb2', 'w2', 'b2', 'g_in', 'be_in', 'm_in', 'v_in', 'g_msg', 'be_msg', 'm_msg', 'v_msg', 'g_upd', 'be_upd', 'm_upd', 'v_upd', 'g_out', 'be_out', 'm_out', 'v_out')}
    del _L0_gnn_all
    return {'x': x, 'src': src, 'dst': dst, 'edge_attr_128': edge_attr_128, 'edge_weight': edge_weight, 'L0_gnn_w1': _L0_gnn_in['w1'], 'L0_gnn_b1': _L0_gnn_in['b1'], 'L0_gnn_kw1': _L0_gnn_in['kw1'], 'L0_gnn_kb1': _L0_gnn_in['kb1'], 'L0_gnn_kw2': _L0_gnn_in['kw2'], 'L0_gnn_kb2': _L0_gnn_in['kb2'], 'L0_gnn_w2': _L0_gnn_in['w2'], 'L0_gnn_b2': _L0_gnn_in['b2'], 'L0_gnn_g_in': _L0_gnn_in['g_in'], 'L0_gnn_be_in': _L0_gnn_in['be_in'], 'L0_gnn_m_in': _L0_gnn_in['m_in'], 'L0_gnn_v_in': _L0_gnn_in['v_in'], 'L0_gnn_g_msg': _L0_gnn_in['g_msg'], 'L0_gnn_be_msg': _L0_gnn_in['be_msg'], 'L0_gnn_m_msg': _L0_gnn_in['m_msg'], 'L0_gnn_v_msg': _L0_gnn_in['v_msg'], 'L0_gnn_g_upd': _L0_gnn_in['g_upd'], 'L0_gnn_be_upd': _L0_gnn_in['be_upd'], 'L0_gnn_m_upd': _L0_gnn_in['m_upd'], 'L0_gnn_v_upd': _L0_gnn_in['v_upd'], 'L0_gnn_g_out': _L0_gnn_in['g_out'], 'L0_gnn_be_out': _L0_gnn_in['be_out'], 'L0_gnn_m_out': _L0_gnn_in['m_out'], 'L0_gnn_v_out': _L0_gnn_in['v_out']}

def reference(x, src, dst, edge_attr_128, edge_weight, L0_gnn_w1, L0_gnn_b1, L0_gnn_kw1, L0_gnn_kb1, L0_gnn_kw2, L0_gnn_kb2, L0_gnn_w2, L0_gnn_b2, L0_gnn_g_in, L0_gnn_be_in, L0_gnn_m_in, L0_gnn_v_in, L0_gnn_g_msg, L0_gnn_be_msg, L0_gnn_m_msg, L0_gnn_v_msg, L0_gnn_g_upd, L0_gnn_be_upd, L0_gnn_m_upd, L0_gnn_v_upd, L0_gnn_g_out, L0_gnn_be_out, L0_gnn_m_out, L0_gnn_v_out):
    import jax
    import jax.numpy as jnp

    def _L0_gnn_ref(x, edge_input, edge_list, edge_weight, w1, b1, kw1, kb1, kw2, kb2, w2, b2, g_in, be_in, m_in, v_in, g_msg, be_msg, m_msg, v_msg, g_upd, be_upd, m_upd, v_upd, g_out, be_out, m_out, v_out):
        import jax, jax.numpy as jnp
        import numpy as np
        BN_EPS = 1e-05

        def _bn(x, gamma, beta, mean, var):
            return (x - mean) / jnp.sqrt(var + BN_EPS) * gamma + beta
        N = x.shape[0]
        H = w1.shape[1]
        node_in = edge_list[:, 0]
        node_out = edge_list[:, 1]
        xn = _bn(x, g_in, be_in, m_in, v_in)
        layer_input = jax.nn.relu(xn)
        msg = layer_input[node_in] @ w1 + b1
        msg = jax.nn.relu(_bn(msg, g_msg, be_msg, m_msg, v_msg))
        kern = jax.nn.relu(edge_input @ kw1 + kb1) @ kw2 + kb2
        kern = kern.reshape(-1, H + 1, H)
        msg = jnp.einsum('ejk,ek->ej', kern[:, 1:, :], msg) + kern[:, 0, :]
        update = jax.ops.segment_sum(msg * edge_weight[:, None], node_out, num_segments=N)
        update = jax.nn.relu(_bn(update, g_upd, be_upd, m_upd, v_upd))
        out = update @ w2 + b2
        out = _bn(out, g_out, be_out, m_out, v_out)
        return out
    edge_index_t = jnp.stack([src, dst], axis=1)
    h = jnp.maximum(_layernorm(x, axis=-1), 0.0)
    x = x + _L0_gnn_ref(h, edge_attr_128, edge_index_t, edge_weight, L0_gnn_w1, L0_gnn_b1, L0_gnn_kw1, L0_gnn_kb1, L0_gnn_kw2, L0_gnn_kb2, L0_gnn_w2, L0_gnn_b2, L0_gnn_g_in, L0_gnn_be_in, L0_gnn_m_in, L0_gnn_v_in, L0_gnn_g_msg, L0_gnn_be_msg, L0_gnn_m_msg, L0_gnn_v_msg, L0_gnn_g_upd, L0_gnn_be_upd, L0_gnn_m_upd, L0_gnn_v_upd, L0_gnn_g_out, L0_gnn_be_out, L0_gnn_m_out, L0_gnn_v_out)
    return x

_drawn_inputs = setup_inputs


def setup_inputs(seed=0):
    import zlib

    import numpy as np

    out = dict(_drawn_inputs(seed))
    spreads = {}
    factors = {'L0_gnn_be_upd': 5.506, 'L0_gnn_m_upd': 5.249}
    for name, (base, spread) in spreads.items():
        noise = np.random.default_rng([zlib.crc32(name.encode()), seed]).standard_normal(out[name].shape)
        drawn = base * np.exp(spread * noise) if base else spread * noise
        out[name] = jnp.asarray(drawn.astype(out[name].dtype))
    for name, factor in factors.items():
        out[name] = (out[name] * factor).astype(out[name].dtype)
    return out
```

```python
import concourse.bass as bass
from concourse import mybir
from contextlib import ExitStack

N, D, E, H, KH, DE = 500, 256, 16500, 64, 32, 128
P = 128
WIN = 7
TILES = -(-E // P)
QT = 4
GQ = 4
GT = QT * GQ
GROUPS = TILES // GT
assert TILES == GROUPS * GT + 1
SLOTS = GT * WIN
SLOTS_LAST = (GT + 1) * WIN
QUADS = GROUPS * GQ + 1
PAIRS = GROUPS * GQ * 2 + 1
C1, K1 = KH + 1, H + 1
NC, NP = 4, N // 4
SWEEPS = -(-N // WIN)
BN_EPS = LN_EPS = 1e-5
LIMIT = ((WIN - 1) / 2) ** 2 + 0.5


def gnn_kernel(nc, x, src, dst, tile_dst, slot_dst, w, ea_t, w1, kw1, kmat, w2, cols, rows, const, out):
    fp32, bf16, fp16, i32 = mybir.dt.float32, mybir.dt.bfloat16, mybir.dt.float16, mybir.dt.int32
    ALU = mybir.AluOpType
    ACT = mybir.ActivationFunctionType
    AX = mybir.AxisListType
    ds = bass.ds

    with ExitStack() as ctx:
        def sb(name, shape, dt=fp32):
            return ctx.enter_context(nc.sbuf_tensor(name, shape, dt))

        def pb(name, shape, dt=fp32):
            return ctx.enter_context(nc.psum_tensor(name, shape, dt))

        def sem(name):
            return ctx.enter_context(nc.semaphore(name))

        xs = sb("xs", [NP, NC, D])
        srcb = sb("srcb", [P, TILES * P], fp16)
        dste = sb("dste", [P, TILES], i32)
        base_i = sb("base_i", [P, TILES], i32)
        slot_i = sb("slot_i", [SLOTS_LAST, GROUPS], i32)
        we = sb("we", [P, TILES])
        ea = sb("ea", [P, GQ, QT * P])
        w1s = sb("w1s", [P, 2, H])
        kw1s = sb("kw1s", [P, KH])
        ks = sb("ks", [K1, C1, H])
        w2s = sb("w2s", [H, D])
        colp = sb("colp", [P, 17])
        rowp = sb("rowp", [K1, 5, D])
        kb1b = sb("kb1b", [P, KH])
        cst = sb("cst", [P, N + P + 2])
        iota_n, ident = cst[:, 0:N], cst[:, N:N + P]
        pcol, lcol = cst[:, N + P:N + P + 1], cst[:, N + P + 1:N + P + 2]

        var = sb("var", [P, 4])
        sd = sb("sd", [P, 4])
        rs = sb("rs", [P, 4])
        nt = sb("nt", [P, 4])
        scl = sb("scl", [P, 4])
        bia = sb("bia", [P, 4])
        varo = sb("varo", [K1, D])
        sdo = sb("sdo", [K1, D])
        rso = sb("rso", [K1, D])
        nto = sb("nto", [K1, D])
        w2e = sb("w2e", [K1, D])
        st = sb("st", [NP, NC, 6])
        mv = sb("mv", [NP, NC, 2])
        lv = sb("lv", [NP, NC])
        lsd = sb("lsd", [NP, NC])
        lrs = sb("lrs", [NP, NC])
        lnt = sb("lnt", [NP, NC])
        lnb = sb("lnb", [NP, NC])
        h = sb("h", [NP, NC, D])
        lit = sb("lit", [P, 2, N])
        mt = sb("mt", [H, N])
        m3 = sb("m3", [NP, NC, 3, H], bf16)
        mrem = sb("mrem", [NP, NC, H])
        mrem2 = sb("mrem2", [NP, NC, H])
        nid = sb("nid", [P, NC])
        base = sb("base", [P, TILES])
        rel = sb("rel", [P, TILES])
        off = sb("off", [P, TILES])
        off2 = sb("off2", [P, TILES])
        worst = sb("worst", [P, 1])
        bad = sb("bad", [P, 1])
        ones = sb("ones", [P, 1])
        flag = sb("flag", [1, 1], i32)
        ohw = sb("ohw", [P, TILES, WIN])
        slot_b = sb("slot_b", [SLOTS_LAST, GROUPS])
        slot_n = sb("slot_n", [SLOTS_LAST, GROUPS])
        oh = sb("oh", [NP, 2, NC, QT * P], bf16)
        gm = sb("gm", [P, 2, QT, K1])
        rsb = sb("rsb", [P, 2, QT, C1])
        rhs = sb("rhs", [P, 2, QT, WIN, C1])
        am = sb("am", [K1, C1, SLOTS_LAST])
        us = sb("us", [SLOTS_LAST, H])
        sel = sb("sel", [SLOTS_LAST, N])
        zer = sb("zer", [1, H + N], bf16)
        upd = sb("upd", [H, N])
        updt = sb("updt", [K1, N])
        outs = sb("outs", [NP, NC, D])

        pf = pb("pf", [P, 2, 512])
        pr = pb("pr", [P, 2, 512])
        pa = pb("pa", [P, 2, 512])
        pu = pb("pu", [P, 512])
        po = pb("po", [P, 512])

        ld = {k: sem("ld_" + k) for k in ("x", "src0", "src1", "dst", "base", "slot", "w", "w1", "kw1", "k", "w2",
                                          "cols", "rows", "kb1", "cst")}
        ea_in = [sem(f"ea_in{i}") for i in range(GQ)]
        dv = sem("dv")
        win_step = sem("win_step")
        stats_ready = sem("stats_ready")
        roots_ready = sem("roots_ready")
        scales_ready = sem("scales_ready")
        h_ready = sem("h_ready")
        hT_ready = sem("hT_ready")
        li_ready = sem("li_ready")
        z_ready = sem("z_ready")
        mt_ready = sem("mt_ready")
        mT_ready = sem("mT_ready")
        m3_ready = sem("m3_ready")
        consts_ready = sem("consts_ready")
        w2e_ready = sem("w2e_ready")
        bad_ready = sem("bad_ready")
        badsum_ready = sem("badsum_ready")
        flag_ready = sem("flag_ready")
        onehot_ready = sem("onehot_ready")
        front_done = sem("front_done")
        gm_ready = sem("gm_ready")
        radd_done = sem("radd_done")
        rhs_ready = sem("rhs_ready")
        back_done = sem("back_done")
        a_ready = sem("a_ready")
        u_done = sem("u_done")
        us_ready = sem("us_ready")
        sel_ready = sem("sel_ready")
        scatter_done = sem("scatter_done")
        sweep_done = sem("sweep_done")
        updt_ready = sem("updt_ready")
        out_mm = sem("out_mm")
        out_ready = sem("out_ready")
        out_sent = sem("out_sent")

        block = ctx.enter_context(nc.Block())

        def sweeps(eng, sweep):
            sweep(0)
            eng.wait_ge(flag_ready, 1)
            missed = eng.value_load(flag[0:1, 0:1], min_val=0, max_val=P)
            with eng.If(missed > 0):
                with eng.Fori(1, SWEEPS + 1) as s:
                    eng.wait_ge(sweep_done, s)
                    sweep(s)
                eng.wait_ge(sweep_done, SWEEPS + 1)
            eng.end_ifs()

        @block.sync
        def _(sp):
            def load_quad(g, q, tiles=QT):
                col = g * (GT * P) + q * (QT * P)
                sp.dma_start(ea[:, q % GQ, 0:tiles * P], ea_t[:, ds(col, tiles * P)]).then_inc(ea_in[q % GQ], 16)

            sp.dma_start(xs[:], x.rearrange("(c p) d -> p c d", p=NP)).then_inc(ld["x"], 16)
            sp.dma_start(colp[:], cols).then_inc(ld["cols"], 16)
            sp.dma_start(cst[:], const).then_inc(ld["cst"], 16)
            sp.dma_start(w1s[:], w1.rearrange("(a p) k -> p a k", p=P)).then_inc(ld["w1"], 16)
            sp.dma_start(kw1s[:], kw1).then_inc(ld["kw1"], 16)

            def sweep(s):
                for q in range(GQ):
                    load_quad(0, q)
                with sp.Fori(0, GROUPS - 1) as g:
                    for q in range(GQ):
                        sp.wait_ge(front_done, s * QUADS + g * GQ + (q + 1))
                        load_quad(g + 1, q)
                sp.wait_ge(front_done, s * QUADS + (GROUPS - 1) * GQ + 1)
                load_quad(GROUPS - 1, GQ, 1)

            sweeps(sp, sweep)
            for c in range(NC):
                sp.wait_ge(out_ready, c + 1)
                sp.dma_start(out[c * NP:(c + 1) * NP, :], outs[:, c, :]).then_inc(out_sent, 16)
            sp.wait_ge(out_sent, 16 * NC)

        @block.gpsimd
        def _(pool):
            half = GT * P
            pool.dma_start(srcb[:, 0:half], src[:, 0:half].to_broadcast([P, half])).then_inc(ld["src0"], 16)
            pool.dma_start(srcb[:, half:], src[:, half:].to_broadcast([P, TILES * P - half])).then_inc(ld["src1"], 16)

        @block.scalar
        def _(act):
            act.dma_start(rowp[:].rearrange("p a d -> p (a d)"),
                          rows[:, 0:5 * D].to_broadcast([K1, 5 * D])).then_inc(ld["rows"], 16)
            act.dma_start(dste[:], dst).then_inc(ld["dst"], 16)
            act.dma_start(base_i[:], tile_dst.to_broadcast([P, TILES])).then_inc(ld["base"], 16)
            act.dma_start(we[:], w).then_inc(ld["w"], 16)
            act.dma_start(slot_i[:], slot_dst).then_inc(ld["slot"], 16)
            act.dma_start(kb1b[:], rows[:, 5 * D:].to_broadcast([P, KH])).then_inc(ld["kb1"], 16)
            act.dma_start(ks[:], kmat).then_inc(ld["k"], 16)
            act.dma_start(w2s[:], w2).then_inc(ld["w2"], 16)

            act.wait_ge(stats_ready, 1)
            nc.scalar.activation(lsd[:], lv[:], ACT.Sqrt)
            nc.scalar.activation(sd[:], var[:], ACT.Sqrt)
            nc.scalar.activation(sdo[:], varo[:], ACT.Sqrt).then_inc(roots_ready, 1)
            act.wait_ge(scales_ready, 1)
            for c in range(NC):
                nc.scalar.activation(h[:, c, :], xs[:, c, :], ACT.Relu, scale=lrs[:, c:c + 1],
                                     bias=lnb[:, c:c + 1]).then_inc(h_ready, 1)
            act.wait_ge(scales_ready, 2)
            act.wait_ge(hT_ready, 1)
            for a in range(2):
                nc.scalar.activation(lit[:, a, :], pr[:, a, 0:N], ACT.Relu, scale=scl[:, a:a + 1],
                                     bias=bia[:, a:a + 1]).then_inc(li_ready, 1)
            act.wait_ge(z_ready, 1)
            nc.scalar.activation(mt[:], pa[0:H, 0, 0:N], ACT.Relu, scale=scl[0:H, 2:3],
                                 bias=bia[0:H, 2:3]).then_inc(mt_ready, 1)
            act.wait_ge(consts_ready, 1)

            def sweep(s):
                q0, p0, g0 = s * QUADS, s * PAIRS, s * GROUPS

                def take_messages(qi, par, tiles=QT, first=False):
                    act.wait_ge(front_done, q0 + (qi + 1))
                    if not first:
                        act.wait_ge(back_done, p0 + (qi - 1) * 2)
                    nc.scalar.copy(gm[:, par, 0:tiles, 0:H],
                                   pf[:, par, 0:tiles * H].rearrange("p (t k) -> p t k", k=H)).then_inc(gm_ready, 1)

                def take_products(qi, q, h, tiles=2):
                    act.wait_ge(back_done, p0 + qi * 2 + (h + 1))
                    for t in range(tiles):
                        slot = (q * QT + 2 * h + t) * WIN
                        ins = nc.scalar.copy(
                            am[:, :, slot:slot + WIN].rearrange("k c l -> k l c"),
                            pa[0:K1, h, t * WIN * C1:(t + 1) * WIN * C1]
                            .rearrange("k (l c) -> k l c", c=C1))
                    ins.then_inc(a_ready, 1)

                def take_slots(g, rows):
                    act.wait_ge(u_done, g0 + (g + 1))
                    nc.scalar.copy(us[0:rows, :], pu[0:rows, 0:H]).then_inc(us_ready, 1)

                def group(g, first=False, last=False):
                    for q in range(GQ):
                        qi = g * GQ + q
                        take_messages(qi + 1, (q + 1) % 2, 1 if last and q == GQ - 1 else QT, first and q == 0)
                        if q == 0 and not first:
                            take_slots(g - 1, SLOTS)
                        take_products(qi, q, 0)
                        take_products(qi, q, 1)

                take_messages(0, 0, first=True)
                group(0, first=True)
                with act.Fori(1, GROUPS - 1) as g:
                    group(g)
                group(GROUPS - 1, last=True)
                take_products(GROUPS * GQ, GQ, 0, 1)
                take_slots(GROUPS - 1, SLOTS_LAST)

            sweeps(act, sweep)
            act.wait_ge(sweep_done, 1)
            nc.scalar.activation(updt[0:H, :], upd[:], ACT.Relu, scale=scl[0:H, 3:4],
                                 bias=bia[0:H, 3:4]).then_inc(updt_ready, 1)

        @block.vector
        def _(dve):
            done = [0]

            def step(ins):
                done[0] += 1
                ins.then_inc(dv, 1)
                dve.wait_ge(dv, done[0])

            def inverse_root(r, s, v, t):
                step(nc.vector.reciprocal(r, s))
                step(nc.vector.tensor_tensor(t, r, r, ALU.mult))
                step(nc.vector.tensor_tensor(t, t, v, ALU.mult))
                step(nc.vector.tensor_scalar(t, t, -0.5, 1.5, ALU.mult, ALU.add))
                step(nc.vector.tensor_tensor(r, r, t, ALU.mult))

            dve.wait_ge(ld["x"], 16)
            for c in range(NC):
                step(nc.vector.bn_stats(st[:, c, :], xs[:, c, :]))
                step(nc.vector.bn_aggr(mv[:, c, :], st[:, c, :]))
            step(nc.vector.tensor_scalar_add(lv[:], mv[:, :, 1], LN_EPS))
            dve.wait_ge(ld["cols"], 16)
            step(nc.vector.tensor_scalar_add(var[:], colp[:, 12:16], BN_EPS))
            dve.wait_ge(ld["rows"], 16)
            nc.vector.tensor_scalar_add(varo[:], rowp[:, 3, :], BN_EPS).then_inc(stats_ready, 1)
            dve.wait_ge(roots_ready, 1)
            dve.wait_ge(stats_ready, 1)
            inverse_root(lrs[:], lsd[:], lv[:], lnt[:])
            step(nc.vector.tensor_tensor(lnb[:], mv[:, :, 0], lrs[:], ALU.mult))
            nc.vector.tensor_scalar_mul(lnb[:], lnb[:], -1.0).then_inc(scales_ready, 1)
            inverse_root(rs[:], sd[:], var[:], nt[:])
            step(nc.vector.tensor_tensor(scl[:], colp[:, 0:4], rs[:], ALU.mult))
            step(nc.vector.tensor_copy(nt[:], colp[:, 8:12]))
            step(nc.vector.tensor_tensor(nt[:, 2:3], colp[:, 10:11], colp[:, 16:17], ALU.subtract))
            step(nc.vector.tensor_tensor(nt[:], nt[:], scl[:], ALU.mult))
            nc.vector.tensor_tensor(bia[:], colp[:, 4:8], nt[:], ALU.subtract).then_inc(scales_ready, 1)

            dve.wait_ge(ld["cst"], 16)
            for c in range(NC):
                nc.vector.tensor_scalar_add(nid[:, c:c + 1], pcol, float(c * NP))
            nc.vector.memset(zer[:], 0.0)
            nc.vector.memset(ones[:], 1.0)
            nc.vector.memset(updt[H:K1, :], 1.0)
            nc.vector.memset(gm[:, :, :, H:K1], 1.0)
            nc.vector.memset(rsb[:, :, :, KH:C1], 1.0).then_inc(consts_ready, 1)

            def slot_weights():
                for l in range(WIN):
                    nc.vector.scalar_tensor_tensor(out=ohw[:, :, l], in0=rel[:], scalar=float(l), in1=we[:],
                                                   op0=ALU.is_equal, op1=ALU.mult)
                return nc.vector.tensor_scalar(slot_n[:], slot_b[:], lcol[0:SLOTS_LAST, :], None, ALU.add)

            for k in ("base", "dst", "w", "slot"):
                dve.wait_ge(ld[k], 16)
            step(nc.vector.tensor_copy(slot_b[:], slot_i[:]))
            step(nc.vector.tensor_copy(base[:], base_i[:]))
            step(nc.vector.tensor_tensor(rel[:], dste[:], base[:], ALU.subtract))
            step(slot_weights())
            mid = (WIN - 1) / 2
            step(nc.vector.tensor_scalar_add(off[:], rel[:], -mid))
            step(nc.vector.tensor_tensor(off2[:], off[:], off[:], ALU.mult))
            step(nc.vector.reduce_max(worst[:], off2[:], AX.X))
            nc.vector.tensor_scalar(bad[:], worst[:], LIMIT, None, ALU.is_gt).then_inc(bad_ready, 1)

            inverse_root(rso[:], sdo[:], varo[:], nto[:])
            step(nc.vector.tensor_tensor(rso[:], rso[:], rowp[:, 0, :], ALU.mult))
            dve.wait_ge(ld["w2"], 16)
            nc.vector.tensor_tensor(w2e[0:H, :], w2s[:], rso[0:H, :], ALU.mult)
            step(nc.vector.tensor_tensor(nto[H:K1, :], rowp[H:K1, 4, :], rowp[H:K1, 2, :], ALU.subtract))
            step(nc.vector.tensor_tensor(nto[H:K1, :], nto[H:K1, :], rso[H:K1, :], ALU.mult))
            nc.vector.tensor_tensor(w2e[H:K1, :], nto[H:K1, :], rowp[H:K1, 1, :], ALU.add).then_inc(w2e_ready, 1)

            dve.wait_ge(badsum_ready, 1)
            nc.vector.tensor_copy(flag[:], pu[0:1, 0:1]).then_inc(flag_ready, 1)

            dve.wait_ge(mT_ready, 1)
            mp = pa[0:NP, 1, 0:NC * H].rearrange("p (c k) -> p c k", k=H)
            step(nc.vector.tensor_copy(m3[:, :, 0, :], mp))
            step(nc.vector.tensor_tensor(mrem[:], mp, m3[:, :, 0, :], ALU.subtract))
            step(nc.vector.tensor_copy(m3[:, :, 1, :], mrem[:]))
            step(nc.vector.tensor_tensor(mrem2[:], mrem[:], m3[:, :, 1, :], ALU.subtract))
            nc.vector.tensor_copy(m3[:, :, 2, :], mrem2[:]).then_inc(m3_ready, 1)
            dve.wait_ge(ld["kb1"], 16)
            dve.wait_ge(consts_ready, 1)

            def sweep(s):
                q0, p0, g0 = s * QUADS, s * PAIRS, s * GROUPS

                def one_hot(g, q, qi, par, tiles=QT, first=False):
                    if not first:
                        dve.wait_ge(front_done, q0 + (qi - 1))
                    col = g * (GT * P) + q * (QT * P)
                    for c in range(NC):
                        ins = nc.vector.tensor_scalar(oh[:, par, c, 0:tiles * P], srcb[0:NP, ds(col, tiles * P)],
                                                      nid[0:NP, c:c + 1], None, ALU.is_equal)
                    ins.then_inc(onehot_ready, 1)

                def edge_layer(g, q, qi, par, tiles=QT, first=False):
                    dve.wait_ge(front_done, q0 + (qi + 1))
                    if not first:
                        dve.wait_ge(rhs_ready, q0 + (qi - 1))
                    nc.vector.tensor_tensor(
                        rsb[:, par, 0:tiles, 0:KH],
                        pr[:, par, 0:tiles * KH].rearrange("p (t c) -> p t c", c=KH),
                        kb1b[:].unsqueeze(1).to_broadcast([P, tiles, KH]), ALU.add).then_inc(radd_done, 1)
                    dve.wait_ge(radd_done, q0 + (qi + 1))
                    if not first:
                        dve.wait_ge(back_done, p0 + (qi - 1) * 2)
                    for t in range(tiles):
                        ins = nc.vector.scalar_tensor_tensor(
                            out=rhs[:, par, t],
                            in0=rsb[:, par, t].unsqueeze(1).to_broadcast([P, WIN, C1]),
                            scalar=0.0,
                            in1=ohw[:, ds(g * GT + (q * QT + t), 1), :].rearrange("p t l -> p (t l)")
                            .unsqueeze(2).to_broadcast([P, WIN, C1]),
                            op0=ALU.max, op1=ALU.mult)
                    ins.then_inc(rhs_ready, 1)

                def slot_nodes(g, rows):
                    dve.wait_ge(scatter_done, g0 + s + (g + 1))
                    nc.vector.tensor_scalar(sel[0:rows, :], iota_n[0:rows, :], slot_n[0:rows, ds(g, 1)], None,
                                            ALU.is_equal).then_inc(sel_ready, 1)

                def group(g, first=False, last=False):
                    for q in range(GQ):
                        qi = g * GQ + q
                        edge_layer(g, q, qi, q % 2, first=first and q < 2)
                        if first and q == 2 and isinstance(s, int):
                            dve.wait_ge(ld["src1"], 16)
                        if not (last and q == GQ - 1):
                            one_hot(g, q + 2, qi + 2, q % 2, 1 if last and q == GQ - 2 else QT)
                        if q == 0 and not first:
                            slot_nodes(g - 1, SLOTS)

                if isinstance(s, int):
                    dve.wait_ge(ld["src0"], 16)
                one_hot(0, 0, 0, 0, first=True)
                one_hot(0, 1, 1, 1, first=True)
                group(0, first=True)
                with dve.Fori(1, GROUPS - 1) as g:
                    group(g)
                group(GROUPS - 1, last=True)
                edge_layer(GROUPS - 1, GQ, GROUPS * GQ, 0, 1)
                slot_nodes(GROUPS - 1, SLOTS_LAST)
                dve.wait_ge(scatter_done, g0 + s + (GROUPS + 1))

            sweep(0)
            nc.vector.tensor_copy(upd[:], po[0:H, 0:N]).then_inc(sweep_done, 1)
            dve.wait_ge(flag_ready, 1)
            missed = dve.value_load(flag[0:1, 0:1], min_val=0, max_val=P)
            with dve.If(missed > 0):
                dve.wait_ge(sweep_done, 1)
                nc.vector.memset(upd[:], 0.0)
                nc.vector.memset(base[:], float(-WIN))
                nc.vector.memset(slot_b[:], float(-WIN)).then_inc(win_step, 1)
                with dve.Fori(1, SWEEPS + 1) as s:
                    dve.wait_ge(sweep_done, s)
                    dve.wait_ge(win_step, s * 3 - 2)
                    nc.vector.tensor_scalar_add(slot_b[:], slot_b[:], float(WIN))
                    nc.vector.tensor_scalar_add(base[:], base[:], float(WIN)).then_inc(win_step, 1)
                    dve.wait_ge(win_step, s * 3 - 1)
                    nc.vector.tensor_tensor(rel[:], dste[:], base[:], ALU.subtract).then_inc(win_step, 1)
                    dve.wait_ge(win_step, s * 3)
                    slot_weights().then_inc(win_step, 1)
                    dve.wait_ge(win_step, s * 3 + 1)
                    sweep(s)
                    nc.vector.tensor_tensor(upd[:], upd[:], po[0:H, 0:N], ALU.add).then_inc(sweep_done, 1)
            dve.end_ifs()

            for c in range(NC):
                dve.wait_ge(out_mm, c + 1)
                nc.vector.tensor_tensor(outs[:, c, :], xs[:, c, :], (pf, pr)[c // 2][0:NP, c % 2, 0:D],
                                        ALU.add).then_inc(out_ready, 1)

        @block.tensor
        def _(pe):
            pe.wait_ge(ld["cst"], 16)
            for c in range(NC):
                pe.wait_ge(h_ready, c + 1)
                for a in range(2):
                    ins = nc.tensor.transpose(pr[:, a, c * NP:(c + 1) * NP], h[:, c, a * P:(a + 1) * P],
                                              ident[0:NP, 0:NP])
            ins.then_inc(hT_ready, 1)
            pe.wait_ge(ld["w1"], 16)
            for a in range(2):
                pe.wait_ge(li_ready, a + 1)
                ins = nc.tensor.matmul(pa[0:H, 0, 0:N], w1s[:, a, :], lit[:, a, :], start=a == 0, stop=a == 1)
            ins.then_inc(z_ready, 1)
            pe.wait_ge(mt_ready, 1)
            for c in range(NC):
                ins = nc.tensor.transpose(pa[0:NP, 1, c * H:(c + 1) * H], mt[:, c * NP:(c + 1) * NP],
                                          ident[0:H, 0:H])
            ins.then_inc(mT_ready, 1)
            pe.wait_ge(consts_ready, 1)
            pe.wait_ge(bad_ready, 1)
            nc.tensor.matmul(pu[0:1, 0:1], bad[:], ones[:], start=True, stop=True).then_inc(badsum_ready, 1)
            pe.wait_ge(m3_ready, 1)
            pe.wait_ge(flag_ready, 1)
            pe.wait_ge(ld["kw1"], 16)
            pe.wait_ge(ld["k"], 16)

            def sweep(s):
                q0, p0, g0 = s * QUADS, s * PAIRS, s * GROUPS

                def front(g, q, qi, par, tiles=QT, first=False):
                    pe.wait_ge(ea_in[q % GQ], (s * (GROUPS + (q % GQ == 0)) + g + (q // GQ + 1)) * 16)
                    pe.wait_ge(onehot_ready, q0 + (qi + 1))
                    if not first:
                        pe.wait_ge(gm_ready, q0 + (qi - 1))
                        pe.wait_ge(radd_done, q0 + (qi - 1))
                    for t in range(tiles):
                        nc.tensor.matmul(pr[:, par, t * KH:(t + 1) * KH],
                                         ea[:, q % GQ, t * P:(t + 1) * P], kw1s[:], start=True, stop=True)
                    for t in range(tiles):
                        for c in range(NC):
                            for part in range(3):
                                ins = nc.tensor.matmul(pf[:, par, t * H:(t + 1) * H],
                                                       oh[:, par, c, t * P:(t + 1) * P], m3[:, c, part, :],
                                                       start=c == 0 and part == 0, stop=c == NC - 1 and part == 2)
                    ins.then_inc(front_done, 1)

                def back(qi, q, h, par, tiles=2, first=False):
                    if h == 0:
                        pe.wait_ge(gm_ready, q0 + (qi + 1))
                        pe.wait_ge(rhs_ready, q0 + (qi + 1))
                    if not first:
                        pe.wait_ge(a_ready, p0 + qi * 2 + (h - 1))
                    for t in range(2 * h, 2 * h + tiles):
                        ins = nc.tensor.matmul(pa[0:K1, h, (t % 2) * WIN * C1:(t % 2 + 1) * WIN * C1],
                                               gm[:, par, t, :], rhs[:, par, t].rearrange("p l c -> p (l c)"),
                                               start=True, stop=True)
                    ins.then_inc(back_done, 1)

                def slot_sums(g, rows, pairs):
                    pe.wait_ge(a_ready, p0 + g * (2 * GQ) + pairs)
                    for c in range(C1):
                        ins = nc.tensor.matmul(pu[0:rows, 0:H], am[:, c, 0:rows], ks[:, c, :],
                                               start=c == 0, stop=c == C1 - 1)
                    ins.then_inc(u_done, 1)

                def scatter(g, rows, last=False):
                    pe.wait_ge(us_ready, g0 + (g + 1))
                    pe.wait_ge(sel_ready, g0 + (g + 1))
                    nc.tensor.matmul(po[0:H, 0:N], us[0:rows, :], sel[0:rows, :], start=False, stop=last,
                                     skip_group_check=True).then_inc(scatter_done, 1)

                def group(g, first=False, last=False):
                    for q in range(GQ):
                        qi = g * GQ + q
                        if last and q == GQ - 1:
                            front(g, GQ, qi + 1, 0, 1)
                        elif q == GQ - 1:
                            front(g + 1, 0, qi + 1, 0)
                        else:
                            front(g, q + 1, qi + 1, (q + 1) % 2, first=first and q == 0)
                        if not first and q == 0:
                            slot_sums(g - 1, SLOTS, 2 * GQ)
                        if not first and q == 1:
                            scatter(g - 1, SLOTS)
                        for h in range(2):
                            back(qi, q, h, q % 2, first=first and q < 1)

                nc.tensor.matmul(po[0:H, 0:N], zer[:, 0:H], zer[:, H:], start=True, stop=False,
                                 skip_group_check=True).then_inc(scatter_done, 1)
                front(0, 0, 0, 0, first=True)
                group(0, first=True)
                with pe.Fori(1, GROUPS - 1) as g:
                    group(g)
                group(GROUPS - 1, last=True)
                back(GROUPS * GQ, GQ, 0, 0, 1)
                slot_sums(GROUPS - 1, SLOTS_LAST, 2 * GQ + 1)
                scatter(GROUPS - 1, SLOTS_LAST, last=True)

            sweeps(pe, sweep)
            pe.wait_ge(updt_ready, 1)
            pe.wait_ge(w2e_ready, 1)
            for c in range(NC):
                nc.tensor.matmul((pf, pr)[c // 2][0:NP, c % 2, 0:D], updt[:, c * NP:(c + 1) * NP], w2e[:],
                                 start=True, stop=True).then_inc(out_mm, 1)


def kernel(x, src, dst, edge_attr_128, edge_weight, **params):
    import numpy as np
    import concourse.bacc as bacc
    from concourse import mybir as mb
    from concourse.bass_utils import run_bass_kernel_spmd

    p = {k[len("L0_gnn_"):]: np.asarray(v) for k, v in params.items()}
    src, dst, w = np.asarray(src), np.asarray(dst), np.asarray(edge_weight)
    pad = TILES * P - E
    dst = np.concatenate([dst, np.repeat(dst[-1:], pad)])
    w = np.concatenate([w, np.zeros(pad, w.dtype)])
    first_edge = (GT * np.arange(GROUPS)[None, :] + np.arange(SLOTS_LAST)[:, None] // WIN) * P
    kern = np.concatenate([p["kw2"], p["kb2"][None]]).reshape(C1, K1, H)
    kmat = np.concatenate([kern[:, 1:, :].transpose(2, 0, 1), kern[None, :, 0, :]])
    wide = lambda v: np.concatenate([v, np.zeros(P - H, v.dtype)])
    cols = [c for k in ("g", "be", "m", "v") for c in
            (p[k + "_in"][:P], p[k + "_in"][P:], wide(p[k + "_msg"]), wide(p[k + "_upd"]))] + [wide(p["b1"])]
    rows = [p[k + "_out"] for k in ("g", "be", "m", "v")] + [p["b2"], p["kb1"]]
    part = np.arange(P)
    const = np.concatenate([np.tile(np.arange(N), (P, 1)), np.eye(P), part[:, None], part[:, None] % WIN],
                           axis=1).astype(np.float32)
    arrays = {
        "x": np.asarray(x),
        "src": np.concatenate([src, np.zeros(pad, src.dtype)])[None, :],
        "dst": dst.reshape(TILES, P).T,
        "tile_dst": dst[None, ::P],
        "slot_dst": dst[first_edge],
        "w": w.reshape(TILES, P).T,
        "ea_t": np.concatenate([np.asarray(edge_attr_128), np.zeros((pad, DE), np.float32)]).T,
        "w1": p["w1"], "kw1": p["kw1"], "kmat": kmat, "w2": p["w2"],
        "cols": np.stack(cols, axis=1), "rows": np.concatenate(rows)[None, :], "const": const,
    }
    arrays = {"in_" + k: np.ascontiguousarray(v) for k, v in arrays.items()}
    nc = bacc.Bacc("TRN2", target_bir_lowering=False, num_devices=1)
    args = [nc.dram_tensor(k, v.shape, mb.dt.from_np(v.dtype), kind="ExternalInput").ap() for k, v in arrays.items()]
    args.append(nc.dram_tensor("out_x", (N, D), mb.dt.float32, kind="ExternalOutput").ap())
    gnn_kernel(nc, *args)
    r = run_bass_kernel_spmd(nc, [arrays], core_ids=[0])
    return r.results[0]["out_x"]
```

```python
import concourse.bass as bass
from concourse import mybir
from contextlib import ExitStack

N, D, E, H, KH, DE = 500, 256, 16500, 64, 32, 128
P = 128
TILES = -(-E // P)
QT = 4
HT = QT // 2
GQ = 4
GT = QT * GQ
GROUPS = TILES // GT
assert TILES == GROUPS * GT + 1
FQUADS = GROUPS * GQ
QUADS = FQUADS + 1
PAIRS = 2 * FQUADS + 1
HALVES = 4
WIN = 2 * HALVES
C1 = KH + 1
RW = HALVES * C1
TW = RW + 2 * HALVES
CA = C1 + 2
AW = N // 2 + HALVES - 1
NC, NP = 4, N // 4
SWEEPS = -(-N // WIN)
EARLY = 2
LEAD = 3
BN_EPS = LN_EPS = 1e-5
MID = (WIN - 1) / 2


def gnn_kernel(nc, x, src_row, src_col, dst, tile_dst, w, ea_t, w1, kw1, kmat, kmat0, w2, cols, rows, const, out):
    fp32, bf16, fp16, i32, u32 = (mybir.dt.float32, mybir.dt.bfloat16, mybir.dt.float16, mybir.dt.int32,
                                  mybir.dt.uint32)
    ALU = mybir.AluOpType
    ACT = mybir.ActivationFunctionType
    AX = mybir.AxisListType
    ds = bass.ds
    table = nc.dram_tensor("m_table", (2 * N, P), fp32).ap()

    with ExitStack() as ctx:
        def sb(name, shape, dt=fp32):
            return ctx.enter_context(nc.sbuf_tensor(name, shape, dt))

        def pb(name, shape, dt=fp32):
            return ctx.enter_context(nc.psum_tensor(name, shape, dt))

        def sem(name):
            return ctx.enter_context(nc.semaphore(name))

        xs = sb("xs", [NP, 2, 2, D])
        srcb = sb("srcb", [P, FQUADS * HT * P], fp16)
        srce = sb("srce", [P, TILES], i32)
        dste = sb("dste", [P, TILES], i32)
        tile_i = sb("tile_i", [P, TILES], i32)
        we = sb("we", [P, TILES])
        ea = sb("ea", [P, LEAD + 1, GT * P])
        ea_last = sb("ea_last", [P, P])
        w1s = sb("w1s", [P, 2, H])
        kw1s = sb("kw1s", [P, KH])
        kbd = sb("kbd", [P, CA, P])
        w2s = sb("w2s", [P, D])
        colp = sb("colp", [P, 17])
        rowp = sb("rowp", [P, 5, D])
        kb1b = sb("kb1b", [P, KH])
        kb1n = sb("kb1n", [P, KH])
        cst = sb("cst", [P, P + 1])
        ident, pcol = cst[:, 0:P], cst[:, P:P + 1]

        var = sb("var", [P, 4])
        sd = sb("sd", [P, 4])
        rs = sb("rs", [P, 4])
        nt = sb("nt", [P, 4])
        scl = sb("scl", [P, 4])
        bia = sb("bia", [P, 4])
        varo = sb("varo", [P, D])
        sdo = sb("sdo", [P, D])
        rso = sb("rso", [P, D])
        nto = sb("nto", [P, D])
        w2e = sb("w2e", [P, D])
        xb = sb("xb", [NP, 2, 2, D])
        st = sb("st", [NP, NC, 6])
        mv = sb("mv", [NP, NC, 2])
        lv = sb("lv", [NP, NC])
        lsd = sb("lsd", [NP, NC])
        lrs = sb("lrs", [NP, NC])
        lnt = sb("lnt", [NP, NC])
        lnb = sb("lnb", [NP, NC])
        h = sb("h", [NP, NC, D])
        lit = sb("lit", [P, 2, N])
        mt = sb("mt", [H, N])
        m3 = sb("m3", [NP, NC, 3, H], bf16)
        mrem = sb("mrem", [NP, NC, H])
        mrem2 = sb("mrem2", [NP, NC, H])
        mtab = sb("mtab", [NP, NC, 2, P])
        nid = sb("nid", [P, NC])
        par_i = sb("par_i", [P, TILES], i32)
        tpar_i = sb("tpar_i", [P, TILES], i32)
        par = sb("par", [P, TILES, 2])
        src2 = sb("src2", [P, TILES], i32)
        base = sb("base", [P, TILES])
        half_f = sb("half_f", [1, TILES + 3])
        half_i = sb("half_i", [1, TILES + 3], i32)
        rel = sb("rel", [P, TILES])
        off = sb("off", [P, TILES])
        off2 = sb("off2", [P, TILES])
        worst = sb("worst", [P, 1])
        bad = sb("bad", [P, 1])
        ones = sb("ones", [P, 1])
        flag = sb("flag", [1, 1], i32)
        wsel = sb("wsel", [P, TILES, 2, HALVES])
        wa = sb("wa", [P, TILES, HALVES])
        rsb = sb("rsb", [P, TILES, KH])
        rq = sb("rq", [P, 2, QT, C1])
        oh = sb("oh", [NP, 2, NC, HT * P], bf16)
        sg = sb("sg", [P, GQ, HT, P])
        sm = sb("sm", [P, 2, HT, 2, H])
        gfix = sb("gfix", [P, GQ, HT], i32)
        rhs = sb("rhs", [P, 2, QT, C1, HALVES])
        prod = sb("prod", [P, GQ, HT, TW])
        am = sb("am", [P, CA, AW])
        updt = sb("updt", [P, N // 2])
        outs = sb("outs", [NP, 2, 2, D])

        pf = pb("pf", [P, 2, 512])
        pr = pb("pr", [P, 2, 512])
        pa = pb("pa", [P, 4, 512])

        ld = {k: sem("ld_" + k) for k in ("x", "src0", "src1", "srce", "dst", "tile", "w", "w1", "kw1", "k", "w2",
                                          "cols", "rows", "kb1", "cst", "ea_last")}
        ea_pre = [sem(f"ea_pre{i}") for i in range(LEAD)]
        ea_in = [sem(f"ea_in{i}") for i in range(GQ)]
        gathered = [sem(f"gathered{i}") for i in range(GQ)]
        dv = sem("dv")
        win_step = sem("win_step")
        cleared = sem("cleared")
        stats_ready = sem("stats_ready")
        roots_ready = sem("roots_ready")
        scales_ready = sem("scales_ready")
        h_ready = sem("h_ready")
        hT_ready = sem("hT_ready")
        li_ready = sem("li_ready")
        z_ready = sem("z_ready")
        mt_ready = sem("mt_ready")
        mT_ready = sem("mT_ready")
        m3_ready = sem("m3_ready")
        mtab_ready = sem("mtab_ready")
        table_sent = sem("table_sent")
        consts_ready = sem("consts_ready")
        bad_ready = sem("bad_ready")
        badsum_ready = sem("badsum_ready")
        flag_ready = sem("flag_ready")
        index_ready = sem("index_ready")
        index_fixed = sem("index_fixed")
        edge_done = sem("edge_done")
        edge_taken = sem("edge_taken")
        r_ready = sem("r_ready")
        onehot_ready = sem("onehot_ready")
        front_done = sem("front_done")
        sm_ready = sem("sm_ready")
        rhs_ready = sem("rhs_ready")
        back_done = sem("back_done")
        prod_ready = sem("prod_ready")
        added = sem("added")
        sweep_done = sem("sweep_done")
        u_done = sem("u_done")
        updt_ready = sem("updt_ready")
        rows_ready = sem("rows_ready")
        w2e_ready = sem("w2e_ready")
        out_mm = sem("out_mm")
        out_ready = sem("out_ready")
        out_sent = sem("out_sent")

        block = ctx.enter_context(nc.Block())

        def sweeps(eng, sweep):
            sweep(0)
            eng.wait_ge(flag_ready, 1)
            missed = eng.value_load(flag[0:1, 0:1], min_val=0, max_val=P)
            with eng.If(missed > 0):
                with eng.Fori(1, SWEEPS + 1) as s:
                    eng.wait_ge(sweep_done, s)
                    sweep(s)
                eng.wait_ge(sweep_done, SWEEPS + 1)
            eng.end_ifs()

        @block.sync
        def _(sp):
            sp.dma_start(xs[:], x.rearrange("(c p b) d -> p c b d", p=NP, b=2)).then_inc(ld["x"], 16)
            sp.dma_start(colp[:], cols).then_inc(ld["cols"], 16)
            sp.dma_start(cst[:], const).then_inc(ld["cst"], 16)
            sp.dma_start(kw1s[:], kw1).then_inc(ld["kw1"], 16)
            sp.dma_start(w1s[:], w1.rearrange("(a p) k -> p a k", p=P)).then_inc(ld["w1"], 16)
            for g in range(LEAD):
                sp.dma_start(ea[:, g, :], ea_t[:, g * GT * P:(g + 1) * GT * P]).then_inc(ea_pre[g], 16)
            sp.dma_start(ea_last[:], ea_t[:, (TILES - 1) * P:]).then_inc(ld["ea_last"], 16)

            def load_quad(g, q):
                col = g * (GT * P) + q * (QT * P)
                sp.dma_start(ea[:, LEAD, q * QT * P:(q + 1) * QT * P],
                             ea_t[:, ds(col, QT * P)]).then_inc(ea_in[q], 16)

            for q in range(GQ):
                load_quad(LEAD, q)
            sp.wait_ge(cleared, 2)
            for b in range(2):
                sp.dma_start(kbd[b * H:(b + 1) * H, 0:C1, b * H:(b + 1) * H], kmat).then_inc(ld["k"], 16)
                sp.dma_start(kbd[0:C1, C1 + b, b * H:(b + 1) * H], kmat0).then_inc(ld["k"], 16)
                sp.dma_start(w2s[b * H:(b + 1) * H, :], w2).then_inc(ld["w2"], 16)
            with sp.Fori(LEAD, GROUPS - 1) as g:
                for q in range(GQ):
                    sp.wait_ge(edge_done, g * GQ + (q + 2))
                    load_quad(g + 1, q)
            rows_of = out.rearrange("(c p b) d -> p c b d", p=NP, b=2)
            for c in range(2):
                sp.wait_ge(out_ready, 2 * c + 2)
                sp.dma_start(rows_of[:, c], outs[:, c]).then_inc(out_sent, 16)
            sp.wait_ge(out_sent, 32)

        @block.gpsimd
        def _(pool):
            half = LEAD * GQ * HT * P
            pool.dma_start(srcb[:, 0:half], src_row[:, 0:half].to_broadcast([P, half])).then_inc(ld["src0"], 16)
            pool.dma_start(srcb[:, half:],
                           src_row[:, half:].to_broadcast([P, FQUADS * HT * P - half])).then_inc(ld["src1"], 16)
            nc.gpsimd.memset(am[:], 0.0).then_inc(cleared, 1)
            nc.gpsimd.memset(kbd[:], 0.0).then_inc(cleared, 1)
            pool.wait_ge(consts_ready, 1)

            def sweep(s):
                q0, p0 = s * QUADS, s * PAIRS
                first_sweep = isinstance(s, int)

                def fix_indices(t0, qi, slot, tiles=HT, first=False):
                    if not first:
                        pool.wait_ge(back_done, p0 + 2 * (qi - 3) - 1)
                    nc.gpsimd.tensor_tensor(gfix[:, slot, 0:tiles], src2[:, ds(t0, tiles)], par_i[:, ds(t0, tiles)],
                                            ALU.add).then_inc(index_fixed, 1)

                def make_r(t0, qi, par, fixed, tiles=QT, first=False):
                    if first_sweep:
                        pool.wait_ge(edge_taken, QUADS if tiles == 1 else qi + 2)
                    if not first:
                        pool.wait_ge(back_done, p0 + 2 * (qi - 1))
                    pool.wait_ge(index_fixed, q0 + fixed)
                    nc.gpsimd.tensor_tensor(rq[:, par, 0:tiles, 0:KH], rsb[:, ds(t0, tiles), :],
                                            kb1b[:].unsqueeze(1).to_broadcast([P, tiles, KH]),
                                            ALU.add).then_inc(r_ready, 1)

                def gather(slot, tiles=HT):
                    for t in range(tiles):
                        pool.indirect_dma_start(
                            out=sg[:, slot, t, :], out_offset=None, in_=table,
                            in_offset=bass.IndirectOffsetOnAxis(ap=gfix[:, slot, t:t + 1].bitcast(u32), axis=0)
                        ).then_inc(gathered[slot], 16)

                def group(g, first=False, last=False):
                    for q in range(GQ):
                        qi, t0 = g * GQ + q, g * GT + q * QT
                        slot, tiles = (q + 3) % GQ, HT
                        if last and q > 0:
                            tiles = 1 if q == 1 else 0
                        if tiles:
                            fix_indices(t0 + 3 * QT, qi + 3, slot, tiles, first and q == 0)
                        make_r(t0 + QT, qi + 1, (q + 1) % 2, qi + 4 if tiles else QUADS,
                               1 if last and q == GQ - 1 else QT, first and q == 0)
                        gather(slot, tiles)

                for q in range(GQ - 1):
                    fix_indices(q * QT, q, q, first=True)
                make_r(0, 0, 0, GQ - 1, first=True)
                if first_sweep:
                    pool.wait_ge(table_sent, 16)
                for q in range(GQ - 1):
                    gather(q)
                group(0, first=True)
                with pool.Fori(1, GROUPS - 1) as g:
                    group(g)
                group(GROUPS - 1, last=True)

            sweeps(pool, sweep)

        @block.scalar
        def _(act):
            act.dma_start(srce[:], src_col).then_inc(ld["srce"], 16)
            act.dma_start(dste[:], dst).then_inc(ld["dst"], 16)
            act.dma_start(tile_i[:], tile_dst.to_broadcast([P, TILES])).then_inc(ld["tile"], 16)
            act.dma_start(we[:], w).then_inc(ld["w"], 16)
            act.dma_start(kb1b[:], rows[:, 5 * D:].to_broadcast([P, KH])).then_inc(ld["kb1"], 16)
            act.dma_start(rowp[:].rearrange("p a d -> p (a d)"),
                          rows[:, 0:5 * D].to_broadcast([P, 5 * D])).then_inc(ld["rows"], 16)

            act.wait_ge(stats_ready, 1)
            nc.scalar.activation(lsd[:], lv[:], ACT.Sqrt)
            nc.scalar.activation(sd[:], var[:], ACT.Sqrt).then_inc(roots_ready, 1)
            act.wait_ge(scales_ready, 1)
            for c in range(NC):
                nc.scalar.activation(h[:, c, :], xs[:, c // 2, c % 2, :], ACT.Relu, scale=lrs[:, c:c + 1],
                                     bias=lnb[:, c:c + 1]).then_inc(h_ready, 1)
            act.wait_ge(scales_ready, 2)
            act.wait_ge(hT_ready, 1)
            for a in range(2):
                nc.scalar.activation(lit[:, a, :], pf[:, a, 0:N], ACT.Relu, scale=scl[:, a:a + 1],
                                     bias=bia[:, a:a + 1]).then_inc(li_ready, 1)
            act.wait_ge(z_ready, 1)
            nc.scalar.activation(mt[:], pa[0:H, 0, 0:N], ACT.Relu, scale=scl[0:H, 2:3],
                                 bias=bia[0:H, 2:3]).then_inc(mt_ready, 1)
            act.wait_ge(mtab_ready, 1)
            act.dma_start(table.rearrange("(c p b2 b) k -> p c (b2 b k)", c=2, b2=2, b=2),
                          mtab[:].rearrange("p (c b2) b k -> p c (b2 b k)", c=2)).then_inc(table_sent, 16)
            act.wait_ge(rows_ready, 1)
            nc.scalar.activation(sdo[:], varo[:], ACT.Sqrt).then_inc(roots_ready, 1)

            def sweep(s):
                f0, p0, t0 = s * FQUADS, s * PAIRS, s * TILES

                def place_messages(qi, tile, pq, first=False):
                    act.wait_ge(front_done, f0 + (qi + 1))
                    if not first:
                        act.wait_ge(back_done, p0 + 2 * (qi - 1))
                    for t in range(HT):
                        for b in range(2):
                            ins = nc.scalar.activation(sm[:, pq, t, b, :], pf[:, pq, t * H:(t + 1) * H], ACT.Copy,
                                                       scale=par[:, ds(tile + t, 1), b])
                    ins.then_inc(sm_ready, 1)

                def take_products(qi, q, h, tiles=HT, first=False):
                    act.wait_ge(back_done, p0 + 2 * qi + (h + 1))
                    if not first:
                        act.wait_ge(added, t0 + QT * (qi - 1))
                    slot = 2 * (q % 2) + h
                    nc.scalar.copy(prod[:, slot, 0:tiles, :].rearrange("p t n -> p (t n)"),
                                   pa[:, slot, 0:tiles * TW]).then_inc(prod_ready, 1)

                def group(g, first=False, last=False):
                    for q in range(GQ):
                        qi, tile = g * GQ + q, g * GT + q * QT
                        if not (last and q == GQ - 1):
                            place_messages(qi + 1, tile + QT + HT, (q + 1) % 2, first and q == 0)
                        for h in range(2):
                            take_products(qi, q, h, first=first and q < 2)

                place_messages(0, HT, 0, first=True)
                group(0, first=True)
                with act.Fori(1, GROUPS - 1) as g:
                    group(g)
                group(GROUPS - 1, last=True)
                take_products(FQUADS, GQ, 0, 1)

            act.wait_ge(index_ready, 1)
            sweeps(act, sweep)
            act.wait_ge(u_done, 1)
            nc.scalar.activation(updt[:], pr[:, 0, 0:N // 2], ACT.Relu, scale=scl[:, 3:4],
                                 bias=bia[:, 3:4]).then_inc(updt_ready, 1)

        @block.vector
        def _(dve):
            done = [0]

            def step(ins):
                done[0] += 1
                ins.then_inc(dv, 1)
                dve.wait_ge(dv, done[0])

            def inverse_root(r, s, v, t):
                step(nc.vector.reciprocal(r, s))
                step(nc.vector.tensor_tensor(t, r, r, ALU.mult))
                step(nc.vector.tensor_tensor(t, t, v, ALU.mult))
                step(nc.vector.tensor_scalar(t, t, -0.5, 1.5, ALU.mult, ALU.add))
                step(nc.vector.tensor_tensor(r, r, t, ALU.mult))

            dve.wait_ge(ld["x"], 16)
            for c in range(NC):
                ins = nc.vector.bn_stats(st[:, c, :], xs[:, c // 2, c % 2, :])
            step(ins)
            for c in range(NC):
                ins = nc.vector.bn_aggr(mv[:, c, :], st[:, c, :])
            step(ins)
            step(nc.vector.tensor_scalar_add(lv[:], mv[:, :, 1], LN_EPS))
            dve.wait_ge(ld["cols"], 16)
            nc.vector.tensor_scalar_add(var[:], colp[:, 12:16], BN_EPS).then_inc(stats_ready, 1)
            dve.wait_ge(roots_ready, 1)
            dve.wait_ge(stats_ready, 1)
            inverse_root(lrs[:], lsd[:], lv[:], lnt[:])
            step(nc.vector.tensor_tensor(lnb[:], mv[:, :, 0], lrs[:], ALU.mult))
            nc.vector.tensor_scalar_mul(lnb[:], lnb[:], -1.0).then_inc(scales_ready, 1)
            inverse_root(rs[:], sd[:], var[:], nt[:])
            step(nc.vector.tensor_tensor(scl[:], colp[:, 0:4], rs[:], ALU.mult))
            step(nc.vector.tensor_copy(nt[:], colp[:, 8:12]))
            step(nc.vector.tensor_tensor(nt[:, 2:3], colp[:, 10:11], colp[:, 16:17], ALU.subtract))
            step(nc.vector.tensor_tensor(nt[:], nt[:], scl[:], ALU.mult))
            nc.vector.tensor_tensor(bia[:], colp[:, 4:8], nt[:], ALU.subtract).then_inc(scales_ready, 1)

            dve.wait_ge(ld["cst"], 16)
            for c in range(NC):
                nc.vector.tensor_scalar(nid[:, c:c + 1], pcol, 2.0, float(2 * NP * (c // 2) + c % 2), ALU.mult, ALU.add)
            nc.vector.memset(ones[:], 1.0)
            nc.vector.memset(mtab[:], 0.0)
            nc.vector.memset(half_f[:], 0.0)
            nc.vector.memset(pa[:, 2:4, 0:HT * TW], 0.0)
            step(nc.vector.memset(rq[:, :, :, KH:C1], 1.0))

            for k in ("srce", "dst", "tile", "w"):
                dve.wait_ge(ld[k], 16)
            step(nc.vector.tensor_single_scalar(par_i[:], dste[:], 1, op=ALU.bitwise_and))
            step(nc.vector.tensor_copy(par[:, :, 1], par_i[:]))
            nc.vector.tensor_scalar(par[:, :, 0], par[:, :, 1], -1.0, 1.0, ALU.mult, ALU.add)
            nc.vector.tensor_scalar_mul(src2[:], srce[:], 2.0)
            step(nc.vector.tensor_single_scalar(tpar_i[:], tile_i[:], 1, op=ALU.bitwise_and))
            step(nc.vector.tensor_tensor(base[:], tile_i[:], tpar_i[:], ALU.subtract))
            step(nc.vector.tensor_scalar_mul(half_f[:, 0:TILES], base[0:1, :], 0.5))
            step(nc.vector.tensor_copy(half_i[:], half_f[:]))
            step(nc.vector.tensor_tensor(rel[:], dste[:], base[:], ALU.subtract))

            def slot_weights():
                for a in range(HALVES):
                    for b in range(2):
                        ins = nc.vector.scalar_tensor_tensor(out=wsel[:, :, b, a], in0=rel[:],
                                                             scalar=float(2 * a + b), in1=we[:],
                                                             op0=ALU.is_equal, op1=ALU.mult)
                return ins

            def half_weights():
                return nc.vector.tensor_tensor(wa[:], wsel[:, :, 0, :], wsel[:, :, 1, :], ALU.add)

            step(slot_weights())
            half_weights().then_inc(index_ready, 1)
            step(nc.vector.tensor_scalar_add(off[:], rel[:], -MID))
            step(nc.vector.tensor_tensor(off2[:], off[:], off[:], ALU.mult))
            step(nc.vector.reduce_max(worst[:], off2[:], AX.X))
            nc.vector.tensor_scalar(bad[:], worst[:], MID * MID + 0.5, None, ALU.is_gt).then_inc(bad_ready, 1)
            dve.wait_ge(ld["kb1"], 16)
            step(nc.vector.tensor_scalar_mul(kb1n[:], kb1b[:], -1.0))
            dve.sem_inc(consts_ready, 1)

            def take_edge_layer(t0, order, pq, tiles=QT):
                dve.wait_ge(edge_done, order + 1)
                nc.vector.tensor_tensor(
                    rsb[:, ds(t0, tiles), :], pr[:, pq, 0:tiles * KH].rearrange("p (t c) -> p t c", c=KH),
                    kb1n[:].unsqueeze(1).to_broadcast([P, tiles, KH]), ALU.max).then_inc(edge_taken, 1)

            for i in range(EARLY):
                take_edge_layer(i * QT, i, i % 2)

            dve.wait_ge(mT_ready, 1)
            mp = pa[0:NP, 1, 0:NC * H].rearrange("p (c k) -> p c k", k=H)
            nc.vector.tensor_copy(mtab[:, :, 0, 0:H], mp)
            nc.vector.tensor_copy(mtab[:, :, 1, H:P], mp).then_inc(mtab_ready, 1)
            step(nc.vector.tensor_copy(m3[:, :, 0, :], mp))
            step(nc.vector.tensor_tensor(mrem[:], mp, m3[:, :, 0, :], ALU.subtract))
            step(nc.vector.tensor_copy(m3[:, :, 1, :], mrem[:]))
            step(nc.vector.tensor_tensor(mrem2[:], mrem[:], m3[:, :, 1, :], ALU.subtract))
            nc.vector.tensor_copy(m3[:, :, 2, :], mrem2[:]).then_inc(m3_ready, 1)
            dve.wait_ge(badsum_ready, 1)
            step(nc.vector.tensor_copy(flag[:], pa[0:1, 0, 0:1]))
            nc.vector.memset(pa[:, 0:2, 0:HT * TW], 0.0).then_inc(flag_ready, 1)
            for i in range(EARLY, LEAD * GQ):
                take_edge_layer(i * QT, i, i % 2)
            take_edge_layer((TILES - 1), LEAD * GQ, (LEAD * GQ) % 2, 1)
            dve.wait_ge(ld["rows"], 16)
            nc.vector.tensor_scalar_add(varo[:], rowp[:, 3, :], BN_EPS).then_inc(rows_ready, 1)

            regs = [dve.alloc_register(f"half{t}") for t in range(QT)]
            dve.wait_ge(cleared, 1)

            def sweep(s):
                f0, q0, p0, a0 = s * FQUADS, s * QUADS, s * PAIRS, s * TILES
                first_sweep = isinstance(s, int)

                def one_hot(qi, pq, first=False):
                    if not first:
                        dve.wait_ge(front_done, f0 + (qi - 1))
                    for c in range(NC):
                        ins = nc.vector.tensor_scalar(oh[:, pq, c, :], srcb[0:NP, ds(qi * (HT * P), HT * P)],
                                                      nid[0:NP, c:c + 1], None, ALU.is_equal)
                    ins.then_inc(onehot_ready, 1)

                def outer(t0, qi, pq, tiles=QT, first=False):
                    dve.wait_ge(r_ready, q0 + (qi + 1))
                    if not first:
                        dve.wait_ge(back_done, p0 + 2 * (qi - 1))
                    nc.vector.tensor_tensor(
                        rhs[:, pq, 0:tiles], rq[:, pq, 0:tiles].unsqueeze(3).to_broadcast([P, tiles, C1, HALVES]),
                        wa[:, ds(t0, tiles), :].unsqueeze(2).to_broadcast([P, tiles, C1, HALVES]),
                        ALU.mult).then_inc(rhs_ready, 1)

                def add(t0, qi, q, tiles=QT, first=False):
                    dve.reg_load(regs[0:tiles], half_i[0:1, ds(t0, tiles)])
                    at = [dve.snap(r, min_val=0, max_val=AW - HALVES) for r in regs[0:tiles]]
                    for t in range(tiles):
                        if t % HT == 0:
                            dve.wait_ge(prod_ready, p0 + 2 * qi + (t // HT + 1))
                        if not (first and t == 0 and first_sweep):
                            dve.wait_ge(added, a0 + QT * qi + t)
                        win = am[:, :, ds(at[t], HALVES)]
                        got = prod[:, 2 * (q % 2) + t // HT, t % HT, :]
                        nc.vector.tensor_tensor(win, win, got.rearrange("p (c a) -> p c a", a=HALVES),
                                                ALU.add).then_inc(added, 1)

                def group(g, first=False, last=False, edge=False):
                    for q in range(GQ):
                        qi, t0 = g * GQ + q, g * GT + q * QT
                        outer(t0 + QT, qi + 1, (q + 1) % 2, 1 if last and q == GQ - 1 else QT, first and q == 0)
                        if first and q == 0 and first_sweep:
                            dve.wait_ge(ld["src1"], 16)
                        if not (last and q >= GQ - 2):
                            one_hot(qi + 2, q % 2)
                        if edge:
                            take_edge_layer(t0 + LEAD * GT, qi + (LEAD * GQ + 1), (q + 1) % 2)
                        add(t0, qi, q, first=first and q == 0)

                if first_sweep:
                    dve.wait_ge(ld["src0"], 16)
                one_hot(0, 0, first=True)
                one_hot(1, 1, first=True)
                outer(0, 0, 0, first=True)
                group(0, first=True, edge=first_sweep)
                if first_sweep:
                    with dve.Fori(1, GROUPS - LEAD) as g:
                        group(g, edge=True)
                    with dve.Fori(GROUPS - LEAD, GROUPS - 1) as g:
                        group(g)
                else:
                    with dve.Fori(1, GROUPS - 1) as g:
                        group(g)
                group(GROUPS - 1, last=True)
                add((TILES - 1), FQUADS, 0, 1)
                dve.wait_ge(added, a0 + TILES)

            sweep(0)
            dve.sem_inc(sweep_done, 1)
            dve.wait_ge(flag_ready, 1)
            missed = dve.value_load(flag[0:1, 0:1], min_val=0, max_val=P)
            with dve.If(missed > 0):
                nc.vector.memset(am[:], 0.0)
                nc.vector.memset(base[:], float(-WIN))
                nc.vector.memset(half_f[:], float(-HALVES)).then_inc(win_step, 1)
                with dve.Fori(1, SWEEPS + 1) as s:
                    dve.wait_ge(sweep_done, s)
                    dve.wait_ge(win_step, s * 4 - 3)
                    nc.vector.tensor_scalar_add(half_f[:], half_f[:], float(HALVES))
                    nc.vector.tensor_scalar_add(base[:], base[:], float(WIN)).then_inc(win_step, 1)
                    dve.wait_ge(win_step, s * 4 - 2)
                    nc.vector.tensor_copy(half_i[:], half_f[:])
                    nc.vector.tensor_tensor(rel[:], dste[:], base[:], ALU.subtract).then_inc(win_step, 1)
                    dve.wait_ge(win_step, s * 4 - 1)
                    slot_weights().then_inc(win_step, 1)
                    dve.wait_ge(win_step, s * 4)
                    half_weights().then_inc(win_step, 1)
                    dve.wait_ge(win_step, s * 4 + 1)
                    sweep(s)
                    dve.sem_inc(sweep_done, 1)
            dve.end_ifs()

            dve.wait_ge(roots_ready, 2)
            inverse_root(rso[:], sdo[:], varo[:], nto[:])
            step(nc.vector.tensor_tensor(rso[:], rso[:], rowp[:, 0, :], ALU.mult))
            dve.wait_ge(ld["w2"], 32)
            nc.vector.tensor_tensor(w2e[:], w2s[:], rso[:], ALU.mult).then_inc(w2e_ready, 1)
            step(nc.vector.tensor_tensor(nto[:], rowp[:, 4, :], rowp[:, 2, :], ALU.subtract))
            step(nc.vector.tensor_tensor(nto[:], nto[:], rso[:], ALU.mult))
            step(nc.vector.tensor_tensor(nto[:], nto[:], rowp[:, 1, :], ALU.add))
            for c in range(NC):
                ins = nc.vector.tensor_tensor(xb[:, c // 2, c % 2, :], xs[:, c // 2, c % 2, :], nto[0:NP, :], ALU.add)
            step(ins)
            for c in range(NC):
                dve.wait_ge(out_mm, c + 1)
                nc.vector.tensor_tensor(outs[:, c // 2, c % 2, :], xb[:, c // 2, c % 2, :],
                                        pa[0:NP, c, 0:D], ALU.add).then_inc(out_ready, 1)

        @block.tensor
        def _(pe):
            def edge_layer(order, ea_quad, pq, tiles=QT, first=False):
                if not first:
                    pe.wait_ge(edge_taken, order - 1)
                for t in range(tiles):
                    ins = nc.tensor.matmul(pr[:, pq, t * KH:(t + 1) * KH], ea_quad[:, t * P:(t + 1) * P], kw1s[:],
                                           start=True, stop=True)
                ins.then_inc(edge_done, 1)

            def early_edge_layer(i):
                if i % GQ == 0:
                    pe.wait_ge(ea_pre[i // GQ], 16)
                edge_layer(i, ea[:, i // GQ, (i % GQ) * QT * P:(i % GQ + 1) * QT * P], i % 2, first=i < 2)

            pe.wait_ge(ld["cst"], 16)
            for c in range(NC):
                pe.wait_ge(h_ready, c + 1)
                for a in range(2):
                    ins = nc.tensor.transpose(pf[:, a, c * NP:(c + 1) * NP], h[:, c, a * P:(a + 1) * P],
                                              ident[0:NP, 0:NP])
            ins.then_inc(hT_ready, 1)
            pe.wait_ge(ld["w1"], 16)
            for a in range(2):
                pe.wait_ge(li_ready, a + 1)
                ins = nc.tensor.matmul(pa[0:H, 0, 0:N], w1s[:, a, :], lit[:, a, :], start=a == 0, stop=a == 1)
            ins.then_inc(z_ready, 1)
            pe.wait_ge(ld["kw1"], 16)
            for i in range(EARLY):
                early_edge_layer(i)
            pe.wait_ge(mt_ready, 1)
            for c in range(NC):
                ins = nc.tensor.transpose(pa[0:NP, 1, c * H:(c + 1) * H], mt[:, c * NP:(c + 1) * NP],
                                          ident[0:H, 0:H])
            ins.then_inc(mT_ready, 1)
            pe.wait_ge(consts_ready, 1)
            pe.wait_ge(bad_ready, 1)
            nc.tensor.matmul(pa[0:1, 0, 0:1], bad[:], ones[:], start=True, stop=True).then_inc(badsum_ready, 1)
            for i in range(EARLY, LEAD * GQ):
                early_edge_layer(i)
            pe.wait_ge(ld["ea_last"], 16)
            edge_layer(LEAD * GQ, ea_last, (LEAD * GQ) % 2, 1)
            pe.wait_ge(m3_ready, 1)
            pe.wait_ge(flag_ready, 1)

            def sweep(s):
                f0, q0, p0 = s * FQUADS, s * QUADS, s * PAIRS
                first_sweep = isinstance(s, int)

                def front(qi, pq, first=False):
                    pe.wait_ge(onehot_ready, f0 + (qi + 1))
                    if not first:
                        pe.wait_ge(sm_ready, f0 + (qi - 1))
                    for t in range(HT):
                        for c in range(NC):
                            for part in range(3):
                                ins = nc.tensor.matmul(pf[:, pq, t * H:(t + 1) * H],
                                                       oh[:, pq, c, t * P:(t + 1) * P], m3[:, c, part, :],
                                                       start=c == 0 and part == 0, stop=c == NC - 1 and part == 2)
                    ins.then_inc(front_done, 1)

                def back(g, qi, q, tiles=QT, first=False):
                    pq, slot = q % 2, q % GQ
                    for t in range(tiles):
                        h = t // HT
                        if t == 0:
                            visits = (g + 1) * (16 * HT) if tiles == QT else GROUPS * 16 * HT + 16
                            pe.wait_ge(gathered[slot], s * (GROUPS * 16 * HT + 16 * (slot == 0)) + visits)
                            pe.wait_ge(rhs_ready, q0 + (qi + 1))
                        if t == HT:
                            pe.wait_ge(sm_ready, f0 + (qi + 1))
                        if t % HT == 0 and not first:
                            pe.wait_ge(prod_ready, p0 + 2 * qi + (h - 3))
                        bank = pa[:, 2 * pq + h, (t % HT) * TW:(t % HT + 1) * TW]
                        messages = sg[:, slot, t, :] if h == 0 else sm[:, pq, t - HT].rearrange("p b k -> p (b k)")
                        nc.tensor.matmul(bank[:, 0:RW], messages, rhs[:, pq, t].rearrange("p c a -> p (c a)"),
                                         start=True, stop=True)
                        ins = nc.tensor.matmul(bank[0:C1, RW:TW], rq[:, pq, t, :],
                                               wsel[:, ds(g * GT + (q * QT + t), 1), :, :]
                                               .rearrange("p t b a -> p (t b a)"), start=True, stop=True)
                        if t % HT == HT - 1 or t == tiles - 1:
                            ins.then_inc(back_done, 1)

                def group(g, first=False, last=False, edge=False):
                    for q in range(GQ):
                        qi = g * GQ + q
                        if not (last and q == GQ - 1):
                            front(qi + 1, (q + 1) % 2, first=first and q == 0)
                        if edge:
                            pe.wait_ge(ea_in[q], (g + 1) * 16)
                            edge_layer(qi + (LEAD * GQ + 1), ea[:, LEAD, q * QT * P:(q + 1) * QT * P], (q + 1) % 2)
                        back(g, qi, q, first=first and q < 2)

                front(0, 0, first=True)
                group(0, first=True, edge=first_sweep)
                if first_sweep:
                    with pe.Fori(1, GROUPS - LEAD) as g:
                        group(g, edge=True)
                    with pe.Fori(GROUPS - LEAD, GROUPS - 1) as g:
                        group(g)
                else:
                    with pe.Fori(1, GROUPS - 1) as g:
                        group(g)
                group(GROUPS - 1, last=True)
                back(GROUPS - 1, FQUADS, GQ, 1)

            sweeps(pe, sweep)
            pe.wait_ge(sweep_done, 1)
            pe.wait_ge(ld["k"], 64)
            for c in range(CA):
                rows_in = P if c < C1 else C1
                ins = nc.tensor.matmul(pr[:, 0, 0:N // 2], kbd[0:rows_in, c, :], am[0:rows_in, c, 0:N // 2],
                                       start=c == 0, stop=c == CA - 1)
            ins.then_inc(u_done, 1)
            pe.wait_ge(updt_ready, 1)
            pe.wait_ge(w2e_ready, 1)
            for c in range(2):
                for b in range(2):
                    nc.tensor.matmul(pa[0:NP, 2 * c + b, 0:D], updt[b * H:(b + 1) * H, c * NP:(c + 1) * NP],
                                     w2e[b * H:(b + 1) * H, :], start=True, stop=True).then_inc(out_mm, 1)


def kernel(x, src, dst, edge_attr_128, edge_weight, **params):
    import numpy as np
    import concourse.bacc as bacc
    from concourse import mybir as mb
    from concourse.bass_utils import run_bass_kernel_spmd

    p = {k[len("L0_gnn_"):]: np.asarray(v) for k, v in params.items()}
    src, dst, w = np.asarray(src), np.asarray(dst), np.asarray(edge_weight)
    pad = TILES * P - E
    src = np.concatenate([src, np.zeros(pad, src.dtype)])
    dst = np.concatenate([dst, np.repeat(dst[-1:], pad)])
    w = np.concatenate([w, np.zeros(pad, w.dtype)])
    kern = np.concatenate([p["kw2"], p["kb2"][None]]).reshape(C1, H + 1, H)
    wide = lambda v: np.concatenate([v, np.zeros(P - H, v.dtype)])
    twice = lambda v: np.concatenate([v, v])
    cols = [c for k in ("g", "be", "m", "v") for c in
            (p[k + "_in"][:P], p[k + "_in"][P:], wide(p[k + "_msg"]), twice(p[k + "_upd"]))] + [wide(p["b1"])]
    rows = [p[k + "_out"] for k in ("g", "be", "m", "v")] + [p["b2"], p["kb1"]]
    arrays = {
        "x": np.asarray(x),
        "src_row": src[:FQUADS * QT * P].reshape(FQUADS, 2, HT * P)[:, 1].reshape(1, -1),
        "src_col": src.reshape(TILES, P).T,
        "dst": dst.reshape(TILES, P).T,
        "tile_dst": dst[None, ::P],
        "w": w.reshape(TILES, P).T,
        "ea_t": np.concatenate([np.asarray(edge_attr_128), np.zeros((pad, DE), np.float32)]).T,
        "w1": p["w1"], "kw1": p["kw1"],
        "kmat": kern[:, 1:, :].transpose(2, 0, 1), "kmat0": kern[:, 0, :], "w2": p["w2"],
        "cols": np.stack(cols, axis=1), "rows": np.concatenate(rows)[None, :],
        "const": np.concatenate([np.eye(P), np.arange(P)[:, None]], axis=1).astype(np.float32),
    }
    arrays = {"in_" + k: np.ascontiguousarray(v) for k, v in arrays.items()}
    nc = bacc.Bacc("TRN2", target_bir_lowering=False, num_devices=1)
    args = [nc.dram_tensor(k, v.shape, mb.dt.from_np(v.dtype), kind="ExternalInput").ap() for k, v in arrays.items()]
    args.append(nc.dram_tensor("out_x", (N, D), mb.dt.float32, kind="ExternalOutput").ap())
    gnn_kernel(nc, *args)
    r = run_bass_kernel_spmd(nc, [arrays], core_ids=[0])
    return r.results[0]["out_x"]
```

```python
import concourse.bass as bass
from concourse import mybir
from contextlib import ExitStack

N, D, E, H, KH, DE = 500, 256, 16500, 64, 32, 128
P = 128
TILES = -(-E // P)
QT = 4
HT = QT // 2
GQ = 4
GT = QT * GQ
GROUPS = TILES // GT
assert TILES == GROUPS * GT + 1
FQUADS = GROUPS * GQ
QUADS = FQUADS + 1
PAIRS = 2 * FQUADS + 1
HALVES = 4
WIN = 2 * HALVES
C1 = KH + 1
RW = HALVES * C1
TW = RW + WIN
ODD_B, MAIN, EVEN_B = 0, 2, C1 + 2
CA = EVEN_B + 2
AW = N // 2 + HALVES - 1
NC, NP = 4, N // 4
SETTLED = 5
UPDATES = (GROUPS - SETTLED) * GQ - 2
UPD_PART = 2
SWEEPS = -(-N // WIN)
LEAD = 4
BEFORE = LEAD + 1
YQ_BEFORE = LEAD * GQ + 1
EDGE_STEPS = BEFORE + GROUPS - LEAD
K_PART = C1 // (GROUPS - 1 - LEAD)
assert K_PART * (GROUPS - 1 - LEAD) == C1
K_LOADS = 16 * (4 + 2 * (GROUPS - 1 - LEAD))
OUT_AFTER = 31
SRC_PARTS = (2 * GQ, 12, 12)
assert sum(SRC_PARTS) == FQUADS
BN_EPS = LN_EPS = 1e-5
MID = (WIN - 1) / 2
COLS = 18
PARAMS = 2 * H + KH + COLS + TILES + P + 1


def gnn_kernel(nc, x, src_row, src_dst, tile_dst, params, ea_t, kmat, kmat0, w2, rows, out):
    fp32, bf16, fp16, i32, u32 = (mybir.dt.float32, mybir.dt.bfloat16, mybir.dt.float16, mybir.dt.int32,
                                  mybir.dt.uint32)
    ALU = mybir.AluOpType
    ACT = mybir.ActivationFunctionType
    AX = mybir.AxisListType
    ds = bass.ds
    table = nc.dram_tensor("m_table", (2 * N, P), fp32).ap()

    with ExitStack() as ctx:
        def sb(name, shape, dt=fp32):
            return ctx.enter_context(nc.sbuf_tensor(name, shape, dt))

        def pb(name, shape, dt=fp32):
            return ctx.enter_context(nc.psum_tensor(name, shape, dt))

        def sem(name):
            return ctx.enter_context(nc.semaphore(name))

        xs = sb("xs", [NP, 2, 2, D])
        srcb = sb("srcb", [P, FQUADS * HT * P], fp16)
        ends = sb("ends", [P, 2, TILES], i32)
        srce, dste = ends[:, 0, :], ends[:, 1, :]
        tile_i = sb("tile_i", [P, TILES], i32)
        ea = sb("ea", [P, LEAD + 1, GT * P])
        ea_last = sb("ea_last", [P, P])
        prm = sb("prm", [P, PARAMS])
        w1s, kw1s, colp, we, ident, pcol = (prm[:, a:b] for a, b in (
            (0, 2 * H),
            (2 * H, 2 * H + KH),
            (2 * H + KH, 2 * H + KH + COLS),
            (PARAMS - P - 1 - TILES, PARAMS - P - 1),
            (PARAMS - P - 1, PARAMS - 1),
            (PARAMS - 1, PARAMS)))
        kb1c = colp[:, COLS - 1:COLS]
        kbd = sb("kbd", [P, CA, P])
        w2s = sb("w2s", [P, D])
        rowp = sb("rowp", [P, 5, D])
        var = sb("var", [P, 4])
        sd = sb("sd", [P, 4])
        rs = sb("rs", [P, 4])
        nt = sb("nt", [P, 4])
        scl = sb("scl", [P, 4])
        bia = sb("bia", [P, 4])
        varo = sb("varo", [P, D])
        sdo = sb("sdo", [P, D])
        rso = sb("rso", [P, D])
        nto = sb("nto", [P, D])
        w2e = sb("w2e", [P, D])
        xb = sb("xb", [NP, 2, 2, D])
        st = sb("st", [NP, NC, 6])
        mv = sb("mv", [NP, NC, 2])
        lv = sb("lv", [NP, NC])
        lsd = sb("lsd", [NP, NC])
        lrs = sb("lrs", [NP, NC])
        lnt = sb("lnt", [NP, NC])
        lnb = sb("lnb", [NP, NC])
        h = sb("h", [NP, NC, D])
        lit = sb("lit", [P, 2, N])
        mt = sb("mt", [H, N])
        m3 = sb("m3", [NP, NC, 3, H], bf16)
        mrem = sb("mrem", [NP, NC, H])
        mrem2 = sb("mrem2", [NP, NC, H])
        mtab = sb("mtab", [NP, NC, 2, P])
        nid = sb("nid", [P, NC, HT * P], fp16)
        par_i = sb("par_i", [P, TILES], i32)
        tpar_i = sb("tpar_i", [P, TILES], i32)
        par = sb("par", [P, TILES, 2])
        src2 = sb("src2", [P, TILES], i32)
        base = sb("base", [P, TILES])
        half_f = sb("half_f", [1, TILES - 1 + GT])
        half_i = sb("half_i", [1, TILES - 1 + GT], i32)
        rel = sb("rel", [P, TILES])
        off = rel
        worst = sb("worst", [P, 1])
        bad = sb("bad", [P, 1])
        back_in = sb("back_in", [P, TILES - SETTLED * GT])
        late = sb("late", [P, 1])
        ones = sb("ones", [P, 1])
        root_of_one = sb("root_of_one", [P, 1])
        flag = sb("flag", [1, 1], i32)
        wsel = sb("wsel", [P, TILES, 2, HALVES])
        wa = sb("wa", [P, TILES, HALVES])
        rsb = sb("rsb", [P, TILES, KH])
        rq = sb("rq", [P, GQ, QT, H])
        oh = sb("oh", [NP, GQ, NC, HT * P], bf16)
        sg = sb("sg", [P, GQ, HT, P])
        sm = sb("sm", [P, 2, HT, 2, H])
        gfix = sb("gfix", [P, GQ, HT], i32)
        rhs = sb("rhs", [P, 2, QT, C1, HALVES])
        prod = sb("prod", [P, GQ, HT * TW])
        am = sb("am", [P, CA, AW])
        updt = lit[:, 0, 0:N // 2]
        outs = h[:].rearrange("p (c b) d -> p c b d", b=2)

        pf = pb("pf", [P, 2, 512])
        pr = pb("pr", [P, 2, 512])
        pa = pb("pa", [P, 4, 512])

        ld = {k: sem("ld_" + k) for k in ("x", "src0", "src1", "src2", "ends", "tile", "k", "w2", "prm", "rows",
                                          "ea_last")}
        ea_pre = [sem(f"ea_pre{i}") for i in range(2 * LEAD)]
        ea_in = [sem(f"ea_in{i}") for i in range(GQ)]
        gathered = [sem(f"gathered{i}") for i in range(GQ)]
        dv = sem("dv")
        win_step = sem("win_step")
        cleared = sem("cleared")
        ones_ready = sem("ones_ready")
        stats_ready = sem("stats_ready")
        roots_ready = sem("roots_ready")
        scales_ready = sem("scales_ready")
        h_ready = sem("h_ready")
        hT_ready = sem("hT_ready")
        li_ready = sem("li_ready")
        z_ready = sem("z_ready")
        mt_ready = sem("mt_ready")
        mT_ready = sem("mT_ready")
        m3_ready = sem("m3_ready")
        mtab_ready = sem("mtab_ready")
        table_sent = sem("table_sent")
        ids_ready = sem("ids_ready")
        bad_ready = sem("bad_ready")
        badsum_ready = sem("badsum_ready")
        flag_ready = sem("flag_ready")
        index_ready = sem("index_ready")
        index_fixed = sem("index_fixed")
        gather_may_start = sem("gather_may_start")
        y_made = sem("y_made")
        y_rectified = sem("y_rectified")
        y_turned = sem("y_turned")
        edge_taken = sem("edge_taken")
        r_ready = sem("r_ready")
        onehot_ready = sem("onehot_ready")
        front_done = sem("front_done")
        sm_ready = sem("sm_ready")
        rhs_ready = sem("rhs_ready")
        back_done = sem("back_done")
        prod_ready = sem("prod_ready")
        added = sem("added")
        sweep_done = sem("sweep_done")
        first_half_made = sem("first_half_made")
        u_done = sem("u_done")
        updt_ready = sem("updt_ready")
        rows_ready = sem("rows_ready")
        w2e_ready = sem("w2e_ready")
        out_mm = sem("out_mm")
        out_ready = sem("out_ready")
        out_sent = sem("out_sent")

        block = ctx.enter_context(nc.Block())

        def y_bank(number):
            return pa[:, number + 1, :] if number in (1, 2) else pr[:, 0, :]

        def sweeps(eng, sweep, after=None):
            sweep(0)
            eng.wait_ge(flag_ready, 1)
            missed = eng.value_load(flag[0:1, 0:1], min_val=0, max_val=P)
            with eng.If(missed > 0):
                with eng.Fori(1, SWEEPS + 1) as s:
                    eng.wait_ge(sweep_done, s)
                    sweep(s)
                eng.wait_ge(sweep_done, SWEEPS + 1)
                if after:
                    after()
            eng.end_ifs()

        @block.sync
        def _(sp):
            sp.dma_start(xs[:], x.rearrange("(c p b) d -> p c b d", p=NP, b=2)).then_inc(ld["x"], 16)
            sp.dma_start(prm[:], params).then_inc(ld["prm"], 16)
            half = GT * P // 2
            for i in range(2 * LEAD):
                if i == 2 * LEAD - 1:
                    sp.dma_start(ea_last[:], ea_t[:, (TILES - 1) * P:]).then_inc(ld["ea_last"], 16)
                    sp.wait_ge(mtab_ready, 1)
                    sp.dma_start(table.rearrange("(c p b2 b) k -> p c (b2 b k)", c=2, b2=2, b=2),
                                 mtab[:].rearrange("p (c b2) b k -> p c (b2 b k)", c=2)).then_inc(table_sent, 16)
                sp.dma_start(ea[:, i // 2, i % 2 * half:(i % 2 + 1) * half],
                             ea_t[:, i * half:(i + 1) * half]).then_inc(ea_pre[i], 16)

            def load_quad(g, q):
                col = g * (GT * P) + q * (QT * P)
                sp.dma_start(ea[:, LEAD, q * QT * P:(q + 1) * QT * P],
                             ea_t[:, ds(col, QT * P)]).then_inc(ea_in[q], 16)

            for q in range(GQ):
                load_quad(LEAD, q)
            sp.wait_ge(gathered[1], 16 * HT)
            sp.dma_start(rowp[:].rearrange("p a d -> p (a d)"),
                         rows[:, 0:5 * D].to_broadcast([P, 5 * D])).then_inc(ld["rows"], 16)
            sp.wait_ge(cleared, 2)
            for b in range(2):
                to = slice(b * H, (b + 1) * H)
                sp.dma_start(kbd[0:C1, EVEN_B + b, to], kmat0).then_inc(ld["k"], 16)
                sp.dma_start(kbd[H:H + C1, ODD_B + b, to], kmat0).then_inc(ld["k"], 16)
                sp.dma_start(w2s[to, :], w2).then_inc(ld["w2"], 16)
            with sp.Fori(LEAD, GROUPS - 1) as g:
                for q in range(GQ):
                    sp.wait_ge(y_made, g * GQ + (q + (YQ_BEFORE - LEAD * GQ + 1)))
                    load_quad(g + 1, q)
                for b in range(2):
                    to = slice(b * H, (b + 1) * H)
                    sp.dma_start(kbd[to, ds(g * K_PART + (MAIN - LEAD * K_PART), K_PART), to],
                                 kmat[:, ds(g * K_PART - LEAD * K_PART, K_PART), :]).then_inc(ld["k"], 16)
            rows_of = out.rearrange("(c p b) d -> p c b d", p=NP, b=2)
            for c in range(2):
                sp.wait_ge(out_ready, 2 * c + 2)
                sp.dma_start(rows_of[:, c], outs[:, c]).then_inc(out_sent, 16)
            sp.wait_ge(out_sent, 32)

        @block.gpsimd
        def _(pool):
            def load_src(part):
                cols = slice(sum(SRC_PARTS[:part]) * HT * P, sum(SRC_PARTS[:part + 1]) * HT * P)
                pool.dma_start(srcb[:, cols], src_row[:, cols].to_broadcast([P, SRC_PARTS[part] * HT * P])
                               ).then_inc(ld[f"src{part}"], 16)

            nc.gpsimd.memset(am[:], 0.0).then_inc(cleared, 1)
            load_src(0)
            nc.gpsimd.memset(kbd[:], 0.0).then_inc(cleared, 1)
            pool.wait_ge(ids_ready, 1)

            def sweep(s):
                q0, p0 = s * QUADS, s * PAIRS
                first_sweep = isinstance(s, int)

                def fix_indices(t0, slot, tiles=HT):
                    nc.gpsimd.tensor_tensor(gfix[:, slot, 0:tiles], src2[:, ds(t0, tiles)], par_i[:, ds(t0, tiles)],
                                            ALU.add).then_inc(index_fixed, 1)

                def wait_to_gather(qi, first=False):
                    pool.wait_ge(index_fixed, q0 + (qi + 1))
                    if not first:
                        pool.wait_ge(back_done, p0 + 2 * (qi - 4) + 1)

                def gather(slot, tiles=HT):
                    for t in range(tiles):
                        pool.indirect_dma_start(
                            out=sg[:, slot, t, :], out_offset=None, in_=table,
                            in_offset=bass.IndirectOffsetOnAxis(ap=gfix[:, slot, t:t + 1].bitcast(u32), axis=0)
                        ).then_inc(gathered[slot], 16)

                def group(g, first=False, last=False):
                    for q in range(GQ):
                        qi, t0 = g * GQ + q, g * GT + q * QT
                        if last and q > 1:
                            continue
                        wait_to_gather(qi + 3, first and q == 0)
                        if last and q == 1:
                            pool.sem_inc(gather_may_start, 1)
                        else:
                            pool.wait_ge(gathered[q], s * (GROUPS * 16 * HT + 16 * (q == 0)) + (g + 1) * (16 * HT))
                            fix_indices(t0 + GQ * QT, q, 1 if last else HT)
                        gather((q + 3) % GQ, 1 if last and q == 1 else HT)
                        if first and first_sweep and q == 1:
                            load_src(2)

                for q in range(GQ):
                    fix_indices(q * QT, q)
                wait_to_gather(GQ - 1, first=True)
                pool.sem_inc(gather_may_start, 1)
                if first_sweep:
                    pool.wait_ge(mtab_ready, 1)
                    load_src(1)
                    pool.wait_ge(table_sent, 16)
                for q in range(GQ - 1):
                    gather(q)
                group(0, first=True)
                with pool.Fori(1, GROUPS - 1) as g:
                    group(g)
                group(GROUPS - 1, last=True)

            sweeps(pool, sweep)

        @block.scalar
        def _(act):
            act.wait_ge(ones_ready, 1)
            nc.scalar.activation(root_of_one[:], ones[:], ACT.Sqrt)
            act.dma_start(ends[:], src_dst).then_inc(ld["ends"], 16)
            act.dma_start(tile_i[:], tile_dst.to_broadcast([P, TILES])).then_inc(ld["tile"], 16)

            def rectify(number, quads, buf, bank, parts=P, width=QT * P):
                act.wait_ge(y_made, quads)
                nc.scalar.activation(buf[0:parts, 0:width], bank[0:parts, 0:width], ACT.Relu,
                                     bias=kb1c[0:parts]).then_inc(y_rectified, 1)

            def store_r(t0, number, tiles=GT):
                act.wait_ge(y_turned, number + 1)
                if tiles == GT:
                    nc.scalar.copy(rsb[:, ds(t0, GT), :].rearrange("p (j i) c -> p i j c", i=QT),
                                   pr[:, 1, :].rearrange("p (i j c) -> p i j c", i=QT, j=GQ)).then_inc(edge_taken, 1)
                else:
                    nc.scalar.copy(rsb[:, t0, :], pr[:, 1, 0:KH]).then_inc(edge_taken, 1)

            act.wait_ge(stats_ready, 1)
            nc.scalar.activation(lsd[:], lv[:], ACT.Sqrt)
            nc.scalar.activation(sd[:], var[:], ACT.Sqrt).then_inc(roots_ready, 1)
            act.wait_ge(scales_ready, 1)
            for c in range(NC):
                nc.scalar.activation(h[:, c, :], xs[:, c // 2, c % 2, :], ACT.Relu, scale=lrs[:, c:c + 1],
                                     bias=lnb[:, c:c + 1]).then_inc(h_ready, 1)
            rectify(0, GQ, ea[:, 0], y_bank(0))
            act.wait_ge(scales_ready, 2)
            act.wait_ge(hT_ready, 1)
            for a in range(2):
                nc.scalar.activation(lit[:, a, :], pf[:, a, 0:N], ACT.Relu, scale=scl[:, a:a + 1],
                                     bias=bia[:, a:a + 1]).then_inc(li_ready, 1)
            act.wait_ge(z_ready, 1)
            nc.scalar.activation(mt[:], pa[0:H, 0, 0:N], ACT.Relu, scale=scl[0:H, 2:3],
                                 bias=bia[0:H, 2:3]).then_inc(mt_ready, 1)
            rectify(1, 2 * GQ, ea[:, 1], y_bank(1))
            store_r(0, 0)

            def sweep(s):
                f0, p0, t0 = s * FQUADS, s * PAIRS, s * TILES
                first_sweep = isinstance(s, int)

                def take_r(tile, qi, slot, tiles=QT, first=False):
                    if not first:
                        act.wait_ge(back_done, p0 + 2 * (qi - 3))
                    nc.scalar.copy(rq[:, slot, 0:tiles, 0:KH], rsb[:, ds(tile, tiles), :]).then_inc(r_ready, 1)

                def place_messages(qi, tile, pq, first=False):
                    act.wait_ge(front_done, f0 + (qi + 1))
                    if not first:
                        act.wait_ge(back_done, p0 + 2 * (qi - 1))
                    for t in range(HT):
                        for b in range(2):
                            ins = nc.scalar.activation(sm[:, pq, t, b, :], pf[:, pq, t * H:(t + 1) * H], ACT.Copy,
                                                       scale=par[:, ds(tile + t, 1), b])
                    ins.then_inc(sm_ready, 1)

                def take_products(qi, q, h, tiles=HT, first=False):
                    act.wait_ge(back_done, p0 + 2 * qi + (h + 1))
                    if not first:
                        act.wait_ge(added, t0 + QT * (qi - 1))
                    slot = 2 * (q % 2) + h
                    nc.scalar.copy(prod[:, slot, 0:tiles * TW], pa[:, slot, 0:tiles * TW]).then_inc(prod_ready, 1)

                def group(g, first=False, last=False, edge=False):
                    act.wait_ge(edge_taken, g + BEFORE if edge else EDGE_STEPS)
                    for q in range(GQ):
                        qi, tile = g * GQ + q, g * GT + q * QT
                        if not (last and q == GQ - 1):
                            place_messages(qi + 1, tile + QT + HT, (q + 1) % 2, first and q == 0)
                            take_r(tile + 2 * QT, qi + 2, (q + 2) % GQ, 1 if last and q == GQ - 2 else QT,
                                   first and q < 2)
                        if edge and q == 2:
                            act.wait_ge(y_turned, g + BEFORE)
                            rectify(g + BEFORE, g * GQ + (YQ_BEFORE + GQ), ea[:, 1], y_bank(0))
                        for h in range(2):
                            take_products(qi, q, h, first=first and q < 2)
                        if edge and q == GQ - 1:
                            store_r(g * GT + LEAD * GT, g + BEFORE)

                act.wait_ge(edge_taken, 1 if first_sweep else EDGE_STEPS)
                for q in range(2):
                    take_r(q * QT, q, q, first=True)
                if first_sweep:
                    for g in range(2, LEAD):
                        rectify(g, (g + 1) * GQ, ea[:, g], y_bank(g))
                        store_r((g - 1) * GT, g - 1)
                    rectify(LEAD, YQ_BEFORE, ea[:, 0], y_bank(LEAD), KH, P)
                place_messages(0, HT, 0, first=True)
                if first_sweep:
                    store_r((LEAD - 1) * GT, LEAD - 1)
                    store_r(TILES - 1, LEAD, 1)
                group(0, first=True, edge=first_sweep)
                if first_sweep:
                    with act.Fori(1, GROUPS - LEAD) as g:
                        group(g, edge=True)
                    with act.Fori(GROUPS - LEAD, GROUPS - 1) as g:
                        group(g)
                else:
                    with act.Fori(1, GROUPS - 1) as g:
                        group(g)
                group(GROUPS - 1, last=True)
                take_products(FQUADS, GQ, 0, 1)

            act.wait_ge(index_ready, 1)
            sweeps(act, sweep)
            act.wait_ge(rows_ready, 1)
            nc.scalar.activation(sdo[:], varo[:], ACT.Sqrt).then_inc(roots_ready, 1)
            for c in range(2):
                act.wait_ge(u_done, c + 1)
                nc.scalar.activation(updt[:, c * NP:(c + 1) * NP], pr[:, c, 0:NP], ACT.Relu, scale=scl[:, 3:4],
                                     bias=bia[:, 3:4]).then_inc(updt_ready, 1)

        @block.vector
        def _(dve):
            done = [0]

            def step(ins):
                done[0] += 1
                ins.then_inc(dv, 1)
                dve.wait_ge(dv, done[0])

            def inverse_root(r, s, v, t):
                step(nc.vector.reciprocal(r, s))
                step(nc.vector.tensor_tensor(t, r, r, ALU.mult))
                step(nc.vector.tensor_tensor(t, t, v, ALU.mult))
                step(nc.vector.tensor_scalar(t, t, -0.5, 1.5, ALU.mult, ALU.add))
                step(nc.vector.tensor_tensor(r, r, t, ALU.mult))

            nc.vector.memset(ones[:], 1.0).then_inc(ones_ready, 1)
            nc.vector.memset(mtab[:], 0.0)
            nc.vector.memset(half_f[:], 0.0)
            step(nc.vector.memset(rq[:], 0.0))
            nc.vector.memset(rq[:, :, :, KH:C1], 1.0)
            dve.wait_ge(ld["x"], 16)
            for c in range(NC):
                ins = nc.vector.bn_stats(st[:, c, :], xs[:, c // 2, c % 2, :])
            step(ins)
            for c in range(NC):
                ins = nc.vector.bn_aggr(mv[:, c, :], st[:, c, :])
            step(ins)
            step(nc.vector.tensor_scalar_add(lv[:], mv[:, :, 1], LN_EPS))
            dve.wait_ge(ld["prm"], 16)
            nc.vector.tensor_scalar_add(var[:], colp[:, 12:16], BN_EPS).then_inc(stats_ready, 1)
            dve.wait_ge(roots_ready, 1)
            dve.wait_ge(stats_ready, 1)
            inverse_root(lrs[:], lsd[:], lv[:], lnt[:])
            step(nc.vector.tensor_tensor(lnb[:], mv[:, :, 0], lrs[:], ALU.mult))
            nc.vector.tensor_scalar_mul(lnb[:], lnb[:], -1.0).then_inc(scales_ready, 1)
            inverse_root(rs[:], sd[:], var[:], nt[:])
            step(nc.vector.tensor_tensor(scl[:], colp[:, 0:4], rs[:], ALU.mult))
            step(nc.vector.tensor_copy(nt[:], colp[:, 8:12]))
            step(nc.vector.tensor_tensor(nt[:, 2:3], colp[:, 10:11], colp[:, 16:17], ALU.subtract))
            step(nc.vector.tensor_tensor(nt[:], nt[:], scl[:], ALU.mult))
            nc.vector.tensor_tensor(bia[:], colp[:, 4:8], nt[:], ALU.subtract).then_inc(scales_ready, 1)

            for c in range(NC):
                nc.vector.tensor_scalar(nid[:, c, :], pcol.to_broadcast([P, HT * P]), 2.0,
                                        float(2 * NP * (c // 2) + c % 2), ALU.mult, ALU.add)

            for k in ("ends", "tile"):
                dve.wait_ge(ld[k], 16)
            step(nc.vector.tensor_single_scalar(par_i[:], dste[:], 1, op=ALU.bitwise_and))
            step(nc.vector.tensor_copy(par[:, :, 1], par_i[:]))
            nc.vector.tensor_scalar(par[:, :, 0], par[:, :, 1], -1.0, 1.0, ALU.mult, ALU.add)
            step(nc.vector.tensor_scalar_mul(src2[:], srce[:], 2.0))
            dve.sem_inc(ids_ready, 1)

            step(nc.vector.tensor_single_scalar(tpar_i[:], tile_i[:], 1, op=ALU.bitwise_and))
            step(nc.vector.tensor_tensor(base[:], tile_i[:], tpar_i[:], ALU.subtract))
            nc.vector.tensor_scalar_mul(half_f[:, 0:SETTLED * GT], base[0:1, 0:SETTLED * GT], 0.5)
            step(nc.vector.tensor_scalar(half_f[:, SETTLED * GT:TILES], base[0:1, SETTLED * GT:], 0.5, float(NP),
                                         ALU.mult, ALU.max))
            step(nc.vector.tensor_copy(half_i[:], half_f[:]))
            step(nc.vector.tensor_tensor(rel[:], dste[:], base[:], ALU.subtract))

            def slot_weights():
                for a in range(HALVES):
                    for b in range(2):
                        ins = nc.vector.scalar_tensor_tensor(out=wsel[:, :, b, a], in0=rel[:],
                                                             scalar=float(2 * a + b), in1=we[:],
                                                             op0=ALU.is_equal, op1=ALU.mult)
                return ins

            def half_weights():
                return nc.vector.tensor_tensor(wa[:], wsel[:, :, 0, :], wsel[:, :, 1, :], ALU.add)

            step(slot_weights())
            dve.wait_ge(mT_ready, 1)
            mp = pa[0:NP, 1, 0:NC * H].rearrange("p (c k) -> p c k", k=H)
            nc.vector.tensor_copy(mtab[:, :, 0, 0:H], mp)
            nc.vector.tensor_copy(mtab[:, :, 1, H:P], mp).then_inc(mtab_ready, 1)
            step(nc.vector.tensor_copy(m3[:, :, 0, :], mp))
            step(nc.vector.tensor_tensor(mrem[:], mp, m3[:, :, 0, :], ALU.subtract))
            step(nc.vector.tensor_copy(m3[:, :, 1, :], mrem[:]))
            step(nc.vector.tensor_tensor(mrem2[:], mrem[:], m3[:, :, 1, :], ALU.subtract))
            nc.vector.tensor_copy(m3[:, :, 2, :], mrem2[:]).then_inc(m3_ready, 1)
            half_weights().then_inc(index_ready, 1)

            step(nc.vector.tensor_scalar_add(off[:], rel[:], -MID))
            step(nc.vector.tensor_tensor(off[:], off[:], off[:], ALU.mult))
            step(nc.vector.reduce_max(worst[:], off[:], AX.X))
            nc.vector.tensor_scalar(back_in[:], base[:, SETTLED * GT:], float(2 * NP), None, ALU.is_lt)
            step(nc.vector.tensor_scalar(bad[:], worst[:], MID * MID + 0.5, None, ALU.is_gt))
            step(nc.vector.reduce_max(late[:], back_in[:], AX.X))
            nc.vector.tensor_tensor(bad[:], bad[:], late[:], ALU.max).then_inc(bad_ready, 1)
            regs = [dve.alloc_register(f"half{t}") for t in range(GT)]
            dve.wait_ge(cleared, 1)

            def sweep(s):
                f0, q0, p0, a0 = s * FQUADS, s * QUADS, s * PAIRS, s * TILES
                first_sweep = isinstance(s, int)

                def one_hot(qi, slot, chunks=range(NC), first=False):
                    if chunks[0] == 0 and not first:
                        dve.wait_ge(front_done, f0 + (qi - 3))
                    n, at = len(chunks), slice(chunks[0], chunks[-1] + 1)
                    ins = nc.vector.tensor_tensor(
                        oh[:, slot, at, :],
                        srcb[0:NP, ds(qi * (HT * P), HT * P)].unsqueeze(1).to_broadcast([NP, n, HT * P]),
                        nid[0:NP, at, :], ALU.is_equal)
                    if chunks[-1] == NC - 1:
                        ins.then_inc(onehot_ready, 1)

                def outer(t0, qi, q, h, tiles=HT, first=False):
                    if h == 0:
                        dve.wait_ge(r_ready, q0 + (qi + 1))
                    if not first:
                        dve.wait_ge(back_done, p0 + 2 * (qi - 2) + (h + 1))
                    at = slice(h * HT, h * HT + tiles)
                    nc.vector.tensor_tensor(
                        rhs[:, q % 2, at], rq[:, q % GQ, at, 0:C1].unsqueeze(3).to_broadcast([P, tiles, C1, HALVES]),
                        wa[:, ds(t0 + h * HT, tiles), :].unsqueeze(2).to_broadcast([P, tiles, C1, HALVES]),
                        ALU.mult).then_inc(rhs_ready, 1)

                def load_places(t0):
                    dve.reg_load(regs[:], half_i[0:1, ds(t0, GT)])

                def places(first, tiles=QT):
                    return [dve.snap(r, min_val=0, max_val=AW - HALVES) for r in regs[first:first + tiles]]

                def add(place, qi, q, t, first=False):
                    if t % HT == 0:
                        dve.wait_ge(prod_ready, p0 + 2 * qi + (t // HT + 1))
                    if not (first and t == 0 and first_sweep):
                        dve.wait_ge(added, a0 + QT * qi + t)
                    blocks = slice(ODD_B, EVEN_B) if t % 2 else slice(MAIN, CA)
                    win = am[:, blocks, ds(place, HALVES)]
                    got = prod[:, 2 * (q % 2) + t // HT, t % HT * TW:(t % HT + 1) * TW]
                    nc.vector.tensor_tensor(win, win, got.rearrange("p (c a) -> p c a", a=HALVES),
                                            ALU.add).then_inc(added, 1)

                def group(g, first=False, last=False):
                    for q in range(GQ):
                        qi, t0 = g * GQ + q, g * GT + q * QT
                        outers = 2 if not last or q < GQ - 2 else 1 if q == GQ - 2 else 0
                        at = places(q * QT)
                        if q == GQ - 1:
                            load_places(g * GT + GT)
                        for t in range(QT):
                            add(at[t], qi, q, t, first and q == 0)
                            if t % HT == 0 and t // HT < outers:
                                outer(t0 + 2 * QT, qi + 2, q + 2, t // HT, HT if outers == 2 else 1)
                            if t % HT == 1 and not last:
                                one_hot(qi + GQ, q, range(t - 1, t + 1))

                if first_sweep:
                    dve.wait_ge(ld["src0"], 16)
                for q in range(2):
                    one_hot(q, q, first=True)
                if first_sweep:
                    dve.wait_ge(badsum_ready, 1)
                    nc.vector.tensor_copy(flag[:], pa[0:1, 0, 0:1]).then_inc(flag_ready, 1)
                for q in range(2, GQ):
                    one_hot(q, q, first=True)
                for q in range(2):
                    for h in range(2):
                        outer(q * QT, q, q, h, first=True)
                load_places(0)
                group(0, first=True)
                if first_sweep:
                    for part in (1, 2):
                        dve.wait_ge(ld[f"src{part}"], 16)
                with dve.Fori(1, GROUPS - 1) as g:
                    group(g)
                group(GROUPS - 1, last=True)
                add(places(0, 1)[0], FQUADS, GQ, 0)
                dve.wait_ge(added, a0 + TILES)

            sweep(0)
            dve.sem_inc(sweep_done, 1)
            dve.wait_ge(flag_ready, 1)
            missed = dve.value_load(flag[0:1, 0:1], min_val=0, max_val=P)
            with dve.If(missed > 0):
                dve.wait_ge(first_half_made, 1)
                nc.vector.memset(am[:], 0.0)
                nc.vector.memset(base[:], float(-WIN))
                nc.vector.memset(half_f[:], float(-HALVES)).then_inc(win_step, 1)
                with dve.Fori(1, SWEEPS + 1) as s:
                    dve.wait_ge(sweep_done, s)
                    dve.wait_ge(win_step, s * 4 - 3)
                    nc.vector.tensor_scalar_add(half_f[:], half_f[:], float(HALVES))
                    nc.vector.tensor_scalar_add(base[:], base[:], float(WIN)).then_inc(win_step, 1)
                    dve.wait_ge(win_step, s * 4 - 2)
                    nc.vector.tensor_copy(half_i[:], half_f[:])
                    nc.vector.tensor_tensor(rel[:], dste[:], base[:], ALU.subtract).then_inc(win_step, 1)
                    dve.wait_ge(win_step, s * 4 - 1)
                    slot_weights().then_inc(win_step, 1)
                    dve.wait_ge(win_step, s * 4)
                    half_weights().then_inc(win_step, 1)
                    dve.wait_ge(win_step, s * 4 + 1)
                    sweep(s)
                    dve.sem_inc(sweep_done, 1)
            dve.end_ifs()

            dve.wait_ge(ld["rows"], 16)
            nc.vector.tensor_scalar_add(varo[:], rowp[:, 3, :], BN_EPS).then_inc(rows_ready, 1)
            dve.wait_ge(roots_ready, 2)
            inverse_root(rso[:], sdo[:], varo[:], nto[:])
            step(nc.vector.tensor_tensor(rso[:], rso[:], rowp[:, 0, :], ALU.mult))
            dve.wait_ge(ld["w2"], 32)
            nc.vector.tensor_tensor(w2e[:], w2s[:], rso[:], ALU.mult).then_inc(w2e_ready, 1)
            step(nc.vector.tensor_tensor(nto[:], rowp[:, 4, :], rowp[:, 2, :], ALU.subtract))
            step(nc.vector.tensor_tensor(nto[:], nto[:], rso[:], ALU.mult))
            step(nc.vector.tensor_tensor(nto[:], nto[:], rowp[:, 1, :], ALU.add))
            for c in range(NC):
                ins = nc.vector.tensor_tensor(xb[:, c // 2, c % 2, :], xs[:, c // 2, c % 2, :], nto[0:NP, :], ALU.add)
            step(ins)
            for c in range(NC):
                dve.wait_ge(out_mm, c + 1)
                nc.vector.tensor_tensor(outs[:, c // 2, c % 2, :], xb[:, c // 2, c % 2, :],
                                        pa[0:NP, c, 0:D], ALU.add).then_inc(out_ready, 1)

        @block.tensor
        def _(pe):
            def edge_quad(j, ea_quad, bank, width=QT * P):
                nc.tensor.matmul(bank[j * KH:(j + 1) * KH, 0:width], kw1s, ea_quad, start=True, stop=True,
                                 tile_position=(0, j * KH)).then_inc(y_made, 1)

            def turn(number, buf, parts=P, tiles=QT):
                pe.wait_ge(y_rectified, number + 1)
                if not isinstance(number, int) or number > 0:
                    pe.wait_ge(edge_taken, number)
                for i in range(tiles):
                    ins = nc.tensor.transpose(pr[:, 1, i * P:i * P + parts], buf[0:parts, i * P:(i + 1) * P],
                                              ident[0:parts, 0:parts])
                ins.then_inc(y_turned, 1)

            def early_quads(g, quads):
                for j in quads:
                    if j % 2 == 0:
                        pe.wait_ge(ea_pre[2 * g + j // 2], 16)
                    edge_quad(j, ea[:, g, j * QT * P:(j + 1) * QT * P], y_bank(g))

            pe.wait_ge(ld["prm"], 16)
            early_quads(0, range(GQ))
            for c in range(NC):
                pe.wait_ge(h_ready, c + 1)
                for a in range(2):
                    ins = nc.tensor.transpose(pf[:, a, c * NP:(c + 1) * NP], h[:, c, a * P:(a + 1) * P],
                                              ident[0:NP, 0:NP])
            ins.then_inc(hT_ready, 1)
            early_quads(1, (0, 1))
            for a in range(2):
                pe.wait_ge(li_ready, a + 1)
                ins = nc.tensor.matmul(pa[0:H, 0, 0:N], w1s[:, a * H:(a + 1) * H], lit[:, a, :],
                                       start=a == 0, stop=a == 1)
            ins.then_inc(z_ready, 1)
            early_quads(1, (2, 3))
            pe.wait_ge(mt_ready, 1)
            for c in range(NC):
                ins = nc.tensor.transpose(pa[0:NP, 1, c * H:(c + 1) * H], mt[:, c * NP:(c + 1) * NP],
                                          ident[0:H, 0:H])
            ins.then_inc(mT_ready, 1)
            turn(0, ea[:, 0])
            for g in range(2, LEAD):
                if g == 3:
                    pe.wait_ge(y_rectified, 1)
                early_quads(g, (0, 1))
                if g == LEAD - 1:
                    pe.wait_ge(bad_ready, 1)
                    nc.tensor.matmul(pa[0:1, 0, 0:1], bad[:], ones[:], start=True, stop=True).then_inc(badsum_ready, 1)
                if g < LEAD - 1:
                    early_quads(g, (2, 3))
                    turn(g - 1, ea[:, g - 1])
            pe.wait_ge(m3_ready, 1)

            def end_early_edge_layer():
                early_quads(LEAD - 1, (2, 3))
                turn(LEAD - 2, ea[:, LEAD - 2])
                pe.wait_ge(y_rectified, LEAD)
                pe.wait_ge(ld["ea_last"], 16)
                edge_quad(0, ea_last[:], y_bank(LEAD), P)
                turn(LEAD - 1, ea[:, LEAD - 1])
                turn(LEAD, ea[:, 0], KH, 1)

            def update(half, blocks):
                for c in blocks:
                    rows = slice(0, P if c < EVEN_B else C1)
                    ins = nc.tensor.matmul(pr[:, half, 0:NP], kbd[rows, c, :],
                                           am[rows, c, half * NP:(half + 1) * NP], start=c == 0, stop=c == CA - 1)
                return ins

            def sweep(s):
                f0, q0, p0 = s * FQUADS, s * QUADS, s * PAIRS
                first_sweep = isinstance(s, int)

                def front(qi, slot, first=False):
                    pe.wait_ge(onehot_ready, f0 + (qi + 1))
                    if not first:
                        pe.wait_ge(sm_ready, f0 + (qi - 1))
                    pq = slot % 2
                    for t in range(HT):
                        for c in range(NC):
                            for part in range(3):
                                ins = nc.tensor.matmul(pf[:, pq, t * H:(t + 1) * H],
                                                       oh[:, slot, c, t * P:(t + 1) * P], m3[:, c, part, :],
                                                       start=c == 0 and part == 0, stop=c == NC - 1 and part == 2)
                    ins.then_inc(front_done, 1)

                def back(g, qi, q, tiles=QT, first=False):
                    pq, slot = q % 2, q % GQ
                    for h in range(-(-tiles // HT)):
                        n = min(tiles, HT)
                        if h == 0:
                            visits = (g + 1) * (16 * HT) if tiles == QT else GROUPS * 16 * HT + 16
                            pe.wait_ge(gathered[slot], s * (GROUPS * 16 * HT + 16 * (slot == 0)) + visits)
                            pe.wait_ge(r_ready, q0 + (qi + 1))
                        else:
                            pe.wait_ge(sm_ready, f0 + (qi + 1))
                        pe.wait_ge(rhs_ready, p0 + 2 * qi + (h + 1))
                        if not first:
                            pe.wait_ge(prod_ready, p0 + 2 * qi + (h - 3))
                        bank = pa[:, 2 * pq + h, :]
                        for i in range(n):
                            messages = sg[:, slot, i, :] if h == 0 else sm[:, pq, i].rearrange("p b k -> p (b k)")
                            at = i * (RW + 2 * WIN)
                            nc.tensor.matmul(bank[:, at:at + RW], messages,
                                             rhs[:, pq, h * HT + i].rearrange("p c a -> p (c a)"),
                                             start=True, stop=True)
                        nc.tensor.matmul(bank[:, RW:RW + n * WIN],
                                         rq[:, slot, h * HT:(h + 1) * HT, :].rearrange("p t c -> p (t c)"),
                                         wsel[:, ds(g * GT + (q * QT + h * HT), n), :, :]
                                         .rearrange("p t b a -> p (t b a)"),
                                         start=True, stop=True).then_inc(back_done, 1)

                def group(g, first=False, last=False, edge=False, updates=False):
                    for q in range(GQ):
                        qi = g * GQ + q
                        if not (last and q == GQ - 1):
                            front(qi + 1, (q + 1) % GQ, first=first and q == 0)
                        if edge:
                            if q == 0:
                                pe.wait_ge(y_rectified, g + BEFORE)
                            if q < 2:
                                for j in (2 * q, 2 * q + 1):
                                    pe.wait_ge(ea_in[j], (g + 1) * 16)
                                    edge_quad(j, ea[:, LEAD, j * QT * P:(j + 1) * QT * P], y_bank(0))
                            if q == GQ - 1:
                                turn(g + BEFORE, ea[:, 1])
                        back(g, qi, q, first=first and q < 2)
                        part = (g - SETTLED) * GQ + q - 2 if updates else -1
                        if part == 0:
                            pe.wait_ge(added, SETTLED * GT)
                            pe.wait_ge(ld["k"], K_LOADS)
                        if part >= 0:
                            update(0, range(part * UPD_PART, (part + 1) * UPD_PART))

                front(0, 0, first=True)
                if first_sweep:
                    end_early_edge_layer()
                    pe.wait_ge(flag_ready, 1)
                group(0, first=True, edge=first_sweep)
                if first_sweep:
                    with pe.Fori(1, GROUPS - LEAD) as g:
                        group(g, edge=True)
                    with pe.Fori(GROUPS - LEAD, SETTLED) as g:
                        group(g)
                    for g in range(SETTLED, GROUPS):
                        group(g, last=g == GROUPS - 1, updates=True)
                else:
                    with pe.Fori(1, GROUPS - 1) as g:
                        group(g)
                    group(GROUPS - 1, last=True)
                back(GROUPS - 1, FQUADS, GQ, 1)
                if first_sweep:
                    update(0, range(UPDATES * UPD_PART, CA)).then_inc(first_half_made, 1)

            sweeps(pe, sweep, after=lambda: update(0, range(CA)))
            pe.wait_ge(sweep_done, 1)

            def out_rows(c):
                pe.wait_ge(updt_ready, c + 1)
                pe.wait_ge(w2e_ready, 1)
                for b in range(2):
                    nc.tensor.matmul(pa[0:NP, 2 * c + b, 0:D], updt[b * H:(b + 1) * H, c * NP:(c + 1) * NP],
                                     w2e[b * H:(b + 1) * H, :], start=True, stop=True).then_inc(out_mm, 1)

            update(1, range(1)).then_inc(u_done, 1)
            update(1, range(1, OUT_AFTER))
            out_rows(0)
            update(1, range(OUT_AFTER, CA)).then_inc(u_done, 1)
            out_rows(1)


def kernel(x, src, dst, edge_attr_128, edge_weight, **params):
    import numpy as np
    import concourse.bacc as bacc
    from concourse import mybir as mb
    from concourse.bass_utils import run_bass_kernel_spmd

    p = {k[len("L0_gnn_"):]: np.asarray(v) for k, v in params.items()}
    src, dst, w = np.asarray(src), np.asarray(dst), np.asarray(edge_weight)
    pad = TILES * P - E
    src = np.concatenate([src, np.zeros(pad, src.dtype)])
    dst = np.concatenate([dst, np.repeat(dst[-1:], pad)])
    w = np.concatenate([w, np.zeros(pad, w.dtype)])
    kern = np.concatenate([p["kw2"], p["kb2"][None]]).reshape(C1, H + 1, H)
    wide = lambda v: np.concatenate([v, np.zeros(P - H, v.dtype)])
    twice = lambda v: np.concatenate([v, v])
    cols = [c for k in ("g", "be", "m", "v") for c in
            (p[k + "_in"][:P], p[k + "_in"][P:], wide(p[k + "_msg"]), twice(p[k + "_upd"]))]
    cols += [wide(p["b1"]), np.tile(p["kb1"], GQ)]
    rows = [p[k + "_out"] for k in ("g", "be", "m", "v")] + [p["b2"]]
    arrays = {
        "x": np.asarray(x),
        "src_row": src[:FQUADS * QT * P].reshape(FQUADS, 2, HT * P)[:, 1].reshape(1, -1),
        "src_dst": np.stack([src.reshape(TILES, P).T, dst.reshape(TILES, P).T], axis=1),
        "tile_dst": dst[None, ::P],
        "params": np.concatenate([p["w1"].reshape(2, P, H).transpose(1, 0, 2).reshape(P, 2 * H), p["kw1"],
                                  np.stack(cols, axis=1), w.reshape(TILES, P).T, np.eye(P, dtype=np.float32),
                                  np.arange(P, dtype=np.float32)[:, None]], axis=1),
        "ea_t": np.concatenate([np.asarray(edge_attr_128), np.zeros((pad, DE), np.float32)]).T,
        "kmat": kern[:, 1:, :].transpose(2, 0, 1), "kmat0": kern[:, 0, :], "w2": p["w2"],
        "rows": np.concatenate(rows)[None, :],
    }
    arrays = {"in_" + k: np.ascontiguousarray(v) for k, v in arrays.items()}
    nc = bacc.Bacc("TRN2", target_bir_lowering=False, num_devices=1)
    args = [nc.dram_tensor(k, v.shape, mb.dt.from_np(v.dtype), kind="ExternalInput").ap() for k, v in arrays.items()]
    args.append(nc.dram_tensor("out_x", (N, D), mb.dt.float32, kind="ExternalOutput").ap())
    gnn_kernel(nc, *args)
    r = run_bass_kernel_spmd(nc, [arrays], core_ids=[0])
    return r.results[0]["out_x"]
```
